# Optimizing a Trainium2 kernel written in Bass

```python
import numpy as np
import jax
import jax.numpy as jnp

def _softmax(x, axis=-1):
    return jax.nn.softmax(x, axis=axis)

def _gelu(x):
    return jax.nn.gelu(x, approximate=True)

def _silu(x):
    return jax.nn.silu(x)

def _sigmoid(x):
    return jax.nn.sigmoid(x)

def _layernorm(x, axis=-1, eps=1e-05):
    m = jnp.mean(x, axis=axis, keepdims=True)
    v = jnp.var(x, axis=axis, keepdims=True)
    return (x - m) / jnp.sqrt(v + eps)

def _scatter_add(tgt, idx, src, axis=0):
    return tgt.at[idx].add(src)

def _segment_sum(src, seg, n):
    return jax.ops.segment_sum(src, seg, n)
kernel_name = 'mk_adj_preln_d2_adj_r2_c11e22'

def setup_inputs(seed: int=0):
    np.random.seed(seed)
    _w = jnp.asarray

    def _rec_inputs():
        import jax
        import jax.numpy as jnp
        _gk = jax.random.key(seed)
        x = -0.000929 + 1 * jax.random.normal(jax.random.fold_in(_gk, 1), (8192, 64), jnp.float32)
        _a = jax.random.bernoulli(jax.random.fold_in(_gk, 2), 0.00195312, (8192, 8192))
        _a = jnp.logical_or(_a, jnp.swapaxes(_a, -1, -2))
        _a = jnp.logical_or(_a, jnp.eye(8192, dtype=bool))
        _af = _a.astype(jnp.float32)
        _af = _af * jax.random.uniform(jax.random.fold_in(_gk, 3), (8192, 8192), jnp.float32, 0.05, 0.0423436)
        adj = _af
        return (x, adj)
    x, adj = _rec_inputs()

    def _L0_gnn_setup():
        import jax, jax.numpy as jnp
        import numpy as np
        N, IN_F, OUT_F, K = (8192, 64, 64, 4)
        key = jax.random.key(seed)
        k1, k2, k3 = jax.random.split(key, 3)
        x = jax.random.normal(k1, (N, IN_F), dtype=jnp.float32)
        L_scaled = jax.random.normal(k2, (N, N), dtype=jnp.float32) / np.sqrt(N)
        fan_in, fan_out = (K * IN_F, OUT_F)
        bound = np.sqrt(6.0 / (fan_in + fan_out))
        weight = jax.random.uniform(k3, (K, IN_F, OUT_F), dtype=jnp.float32, minval=-bound, maxval=bound)
        bias = jnp.zeros((OUT_F,), dtype=jnp.float32)
        return {'x': x, 'L_scaled': L_scaled, 'weight': weight, 'bias': bias}
    _L0_gnn_all = _L0_gnn_setup()
    _L0_gnn_in = {k: v for k, v in _L0_gnn_all.items() if k in ('weight', 'bias')}
    del _L0_gnn_all

    def _L1_gnn_setup():
        import jax, jax.numpy as jnp
        import numpy as np
        EPS = 1e-08

        def poincare_expmap(v, c):
            sc = jnp.sqrt(c)
            norm = jnp.linalg.norm(v, axis=-1, keepdims=True)
            norm = jnp.clip(norm, 0.0, 10.0)
            return jnp.tanh(sc * norm) * v / (sc * norm + EPS)

        def poincare_logmap(y, c):
            sc = jnp.sqrt(c)
            norm = jnp.linalg.norm(y, axis=-1, keepdims=True)
            norm = jnp.clip(norm, 0.0, 0.999)
            return jnp.arctanh(sc * norm) * y / (sc * norm + EPS)
        key = jax.random.key(seed)
        k1, k2, k3 = jax.random.split(key, 3)
        N, F, U = (8192, 64, 64)
        x = jax.random.normal(k1, (N, F), dtype=jnp.float32)
        adj = jax.random.uniform(k2, (N, N), dtype=jnp.float32)
        kernel = jax.random.normal(k3, (F, U), dtype=jnp.float32)
        kernel = kernel / (jnp.linalg.norm(kernel, axis=0, keepdims=True) + EPS)
        bias = jnp.zeros((U,), dtype=jnp.float32)
        return {'x': x, 'adj': adj, 'kernel': kernel, 'bias': bias}
    _L1_gnn_all = _L1_gnn_setup()
    _L1_gnn_in = {k: v for k, v in _L1_gnn_all.items() if k in ('kernel', 'bias')}
    del _L1_gnn_all
    return {'x': x, 'adj': adj, 'L0_gnn_weight': _L0_gnn_in['weight'], 'L0_gnn_bias': _L0_gnn_in['bias'], 'L1_gnn_kernel': _L1_gnn_in['kernel'], 'L1_gnn_bias': _L1_gnn_in['bias']}

def reference(x, adj, L0_gnn_weight, L0_gnn_bias, L1_gnn_kernel, L1_gnn_bias):
    import jax
    import jax.numpy as jnp

    def _L0_gnn_ref(x, L_scaled, weight, bias):
        import jax, jax.numpy as jnp
        import numpy as np
        N, IN_F, OUT_F, K = (8192, 64, 64, 4)
        Tx_prev2 = x
        Tx_prev1 = L_scaled @ x
        out = Tx_prev2 @ weight[0]
        if K > 1:
            out = out + Tx_prev1 @ weight[1]
        for k in range(2, K):
            Tx_curr = 2.0 * (L_scaled @ Tx_prev1) - Tx_prev2
            out = out + Tx_curr @ weight[k]
            Tx_prev2, Tx_prev1 = (Tx_prev1, Tx_curr)
        return out + bias

    def _L1_gnn_ref(x, adj, kernel, bias):
        import jax, jax.numpy as jnp
        import numpy as np
        EPS = 1e-08

        def poincare_expmap(v, c):
            sc = jnp.sqrt(c)
            norm = jnp.linalg.norm(v, axis=-1, keepdims=True)
            norm = jnp.clip(norm, 0.0, 10.0)
            return jnp.tanh(sc * norm) * v / (sc * norm + EPS)

        def poincare_logmap(y, c):
            sc = jnp.sqrt(c)
            norm = jnp.linalg.norm(y, axis=-1, keepdims=True)
            norm = jnp.clip(norm, 0.0, 0.999)
            return jnp.arctanh(sc * norm) * y / (sc * norm + EPS)
        c = 1.0
        x_proj = poincare_expmap(x, c)
        support = adj @ x_proj
        out = poincare_logmap(support, c)
        return out @ kernel + bias
    h = jnp.maximum(_layernorm(x, axis=-1), 0.0)
    x = x + _L0_gnn_ref(h, adj, L0_gnn_weight, L0_gnn_bias)
    h = jnp.maximum(_layernorm(x, axis=-1), 0.0)
    x = x + _L1_gnn_ref(h, adj, L1_gnn_kernel, L1_gnn_bias)
    return x

_drawn_inputs = setup_inputs


def setup_inputs(seed=0):
    import zlib

    import numpy as np

    out = dict(_drawn_inputs(seed))
    spreads = {'L0_gnn_bias': (0.0, 0.1), 'L1_gnn_bias': (0.0, 0.294)}
    factors = {}
    for name, (base, spread) in spreads.items():
        noise = np.random.default_rng([zlib.crc32(name.encode()), seed]).standard_normal(out[name].shape)
        drawn = base * np.exp(spread * noise) if base else spread * noise
        out[name] = jnp.asarray(drawn.astype(out[name].dtype))
    for name, factor in factors.items():
        out[name] = (out[name] * factor).astype(out[name].dtype)
    return out
```

```python
import concourse.bass as bass
from concourse import mybir
from contextlib import ExitStack


def chebyshev_hyperbolic_kernel(nc, x, adj_blocks, cheb_weight, cheb_bias, hyp_kernel, hyp_bias, out):
    fp32 = mybir.dt.float32
    bf16 = mybir.dt.bfloat16
    ALU = mybir.AluOpType
    ACT = mybir.ActivationFunctionType
    AX = mybir.AxisListType

    P = 128
    F = x.shape[2]
    CHUNKS = x.shape[1]
    C = 4
    BLOCK = C * P
    NB = CHUNKS // C
    M = 4
    NM = NB // M
    SWEEPS = 4
    LAST = SWEEPS - 1
    LN_EPS = 1e-5
    EPS = 1e-8
    MAX_NORM = 10.0
    MAX_RADIUS = 0.999
    SERIES_BELOW = 0.25

    H, T1, T2, XP = range(4)
    LEFT = [H, T1, T2, XP]

    DOWN = [True, False, True, False]

    def macro_of(sweep, it):
        return it if DOWN[sweep] else NM - 1 - it

    def row_in_macro(sweep, rt):
        return rt if DOWN[sweep] else M - 1 - rt

    def near_before_far(sweep, rt):
        r = row_in_macro(sweep, rt)
        if sweep in (0, LAST):
            return [(j, False) for j in range(r, M)]
        return [(r, False)]

    def near_after_far(sweep, rt):
        r = row_in_macro(sweep, rt)
        if sweep == 1:
            return [(j, True) for j in range(M - 1, r, -1)]
        return [(j, True) for j in range(r)] if sweep != LAST else []

    def far_parts(sweep, it):
        if sweep == 0:
            return [(it, lambda g: g, True), (NM - 1 - it, lambda g: it + 1 + g, False)]
        return [(it, lambda g: g, sweep != LAST)]

    def uses_before(sweep, it, slot):
        near = sum(len(near_before_far(sweep, r)) + len(near_after_far(sweep, r)) for r in range(M))
        near = -(-(near - slot) // M)
        if sweep == 0:
            return it * (near + M * (NM - 1))
        start = NM * (NM * M) + (sweep - 1) * (NM * near + M * NM * (NM - 1) // 2)
        return start + it * (near - M // 2) + it * it * (M // 2)

    def blocks_of_row(e, sweep, it, rt, ring, block, after_first, after_far):
        def visit(position, groups, mt, off, paired):
            slot = position % M
            uses = e.snap(ring["before"][slot] + groups + position // M)
            e.compute_val(uses + 1)
            block(slot, uses, mt, off, paired)

        def near(parts, groups):
            for off, paired in parts:
                visit(ring["position"], groups, it, off, paired)
                ring["position"] += 1

        in_row = NM - 1 if sweep == 0 else it
        groups = in_row * rt
        first = near_before_far(sweep, rt)
        near(first[:1], groups)
        after_first()
        near(first[1:], groups)
        done = groups
        for count, nth, paired in far_parts(sweep, it):
            with e.If(count > 0):
                with e.Fori(0, count) as g:
                    mt = nc.s_assert_within(nth(g), 0, NM - 1, skip_runtime_bounds_check_because=
                                            "the far columns end at the last macro column")
                    for k in range(M):
                        visit(ring["position"] + k, done + g, mt, k if DOWN[sweep] else M - 1 - k, paired)
            done = done + it
        after_far()
        near(near_after_far(sweep, rt), groups + in_row)

    def macro_rows(e, sweep, row):
        with e.Fori(0, NM) as it:
            ring = {"position": 0, "before": [e.snap(uses_before(sweep, it, s)) for s in range(M)]}
            for rt in range(M):
                row(it, rt, ring)

    def nothing():
        pass

    ctx = ExitStack()
    with ctx:
        def sb(name, shape, dt=fp32):
            return ctx.enter_context(nc.sbuf_tensor(name, shape, dt))

        def pb(name, shape):
            return ctx.enter_context(nc.psum_tensor(name, shape, fp32))

        def sem(name):
            return ctx.enter_context(nc.semaphore(name))

        nodes = sb("nodes", [P, CHUNKS, 4, F])
        resid = sb("resid", [P, CHUNKS, F])
        ring_a = sb("ring_a", [P, M, C, BLOCK])
        staged_w = sb("staged_w", [P, M, C, 2 * F])
        acc_a = sb("acc_a", [P, BLOCK])
        acc_b = sb("acc_b", [P, BLOCK])
        row_vectors = sb("row_vectors", [P, C, 4, F])
        row_turned = sb("row_turned", [P, 2, BLOCK])
        ident = sb("ident", [P, P])
        zeros = sb("zeros", [P, BLOCK], bf16)
        w_raw = sb("w_raw", [P, 4, F])
        w_ht1 = sb("w_ht1", [P, F])
        w_t2u3 = sb("w_t2u3", [P, F])
        w_pair = sb("w_pair", [P, 2 * F])
        w_u3u3 = sb("w_u3u3", [P, F])
        bias = sb("bias", [P, 2, F])
        tmp = sb("tmp", [P, 3, C, F])
        small = sb("small", [P, 12, C])
        result = sb("result", [P, 2, C, F])

        bank_a = [pb(f"bank_a{i}", [P, BLOCK]) for i in range(2)]
        bank_b = [pb(f"bank_b{i}", [P, BLOCK]) for i in range(2)]
        turned_a = pb("turned_a", [P, C, P])
        turned_b = pb("turned_b", [P, C, P])
        proj = [pb(f"proj{i}", [P, C, 2 * F]) for i in range(2)]

        s_x = [sem(f"x_landed{i}") for i in range(NM)]
        s_w = sem("weights_landed")
        s_ident0 = sem("ident_zeroed")
        s_const = sem("constants_ready")
        s_weights = sem("weights_ready")
        s_landed = [sem(f"block_landed{i}") for i in range(M)]
        s_staged = [sem(f"weights_staged{i}") for i in range(M)]
        s_used = [sem(f"slot_used{i}") for i in range(M)]
        s_h = sem("h_ready")
        s_acc = sem("row_accumulated")
        s_evac = sem("row_evacuated")
        s_turned = sem("row_turned_back")
        s_read = sem("turned_read")
        s_final = sem("row_final")
        s_copied = sem("row_copied")
        s_vturned = sem("vectors_turned")
        s_vready = sem("vectors_turned_ready")
        s_var = sem("variance_ready")
        s_std = sem("deviation_ready")
        s_square = sem("norm_squared_ready")
        s_root = sem("norm_root_ready")
        s_norm = sem("norm_ready")
        s_func = sem("function_ready")
        s_chain = sem("vector_chain")
        s_result = sem("result_ready")
        s_out = [sem(f"result_stored{i}") for i in range(2)]

        block = ctx.enter_context(nc.Block())

        def done_before(sweep, it, rt):
            return sweep * NB + it * M + rt

        def order(sweep, mt, off):
            return mt * M + (off if DOWN[sweep] else M - 1 - off) + 1

        @block.sync
        def _(sp):
            for sweep in range(SWEEPS):
                def row(it, rt, ring):
                    i = sp.snap(macro_of(sweep, it) * M + row_in_macro(sweep, rt))

                    def load(slot, uses, mt, off, paired):
                        at = sp.snap((i * NB + macro_of(sweep, mt) * M + off) * P)
                        sp.compute_val(at)
                        sp.wait_ge(s_const, 1)
                        sp.wait_ge(s_used[slot], uses + 1)
                        sp.dma_start(ring_a[:, slot, :, :], adj_blocks[bass.ds(at, P), :, :])\
                            .then_inc(s_landed[slot], 16)

                    blocks_of_row(sp, sweep, it, rt, ring, load, nothing, nothing)
                macro_rows(sp, sweep, row)

        @block.gpsimd
        def _(pool):
            nc.gpsimd.memset(zeros[:, :], 0.0)
            nc.gpsimd.memset(ident[:, :], 0.0).then_inc(s_ident0, 1)
            pool.wait_ge(s_ident0, 1)
            nc.gpsimd.affine_select(out=ident[:, :], in_=ident[:, :], compare_op=ALU.not_equal, fill=1.0,
                                    base=0, pattern=[[-1, P]], channel_multiplier=1).then_inc(s_const, 1)

            for sweep in range(SWEEPS):
                def row(it, rt, ring):
                    def stage(slot, uses, mt, off, paired):
                        J = pool.snap(macro_of(sweep, mt) * M + off)
                        left = LEFT[sweep]
                        if sweep == 0 and not paired:
                            known, count = s_h, order(sweep, mt, off) + 1
                        elif paired:
                            known, count = s_final, sweep * NB + order(sweep, mt, off) + 1
                        else:
                            known, count = s_final, sweep * NB + 1
                        pool.compute_val(count)
                        pool.wait_ge(s_const, 1)
                        pool.wait_ge(known, count)
                        pool.wait_ge(s_used[slot], uses + 1)
                        width = 2 if paired else 1
                        nc.gpsimd.tensor_copy(
                            staged_w[:, slot, :, 0:width * F].rearrange("p c (w f) -> p c w f", w=width),
                            nodes[:, bass.ds(J * C, C), left:left + width, :]).then_inc(s_staged[slot], 1)

                    blocks_of_row(pool, sweep, it, rt, ring, stage, nothing, nothing)
                macro_rows(pool, sweep, row)

        @block.tensor
        def _(pe):
            for s in s_used + [s_turned, s_vturned]:
                pe.sem_inc(s, 1)
            pe.wait_ge(s_const, 1)

            def turn_row(sweep, it, rt):
                rows = pe.snap(done_before(sweep, it, rt))
                half = proj[rt % 2]
                pe.wait_ge(s_evac, rows + 3)
                pe.wait_ge(s_read, rows + 1)
                if sweep != LAST:
                    for c in range(C):
                        last = nc.tensor.transpose(turned_a[:, c, :], acc_a[:, c * P:(c + 1) * P], ident[:, :])
                if sweep != 2:
                    for c in range(C):
                        last = nc.tensor.transpose(turned_b[:, c, :], acc_b[:, c * P:(c + 1) * P], ident[:, :])
                if sweep == 2:
                    for c in range(C):
                        nc.tensor.matmul(half[:, c, :], acc_a[:, c * P:(c + 1) * P], w_pair[:, :],
                                         start=False, stop=False, skip_group_check=True)
                        last = nc.tensor.matmul(half[:, c, 0:F], acc_b[:, c * P:(c + 1) * P], w_u3u3[:, :],
                                                start=False, stop=True, skip_group_check=True)
                if sweep == LAST:
                    pe.wait_ge(s_final, rows)
                    for c in range(C):
                        last = nc.tensor.matmul(half[:, c, 0:F], acc_b[:, c * P:(c + 1) * P], w_raw[:, 3, :],
                                                start=(c == 0), stop=True, skip_group_check=True)
                last.then_inc(s_turned, 1)

            for sweep in range(SWEEPS):
                def row(it, rt, ring):
                    rows = pe.snap(done_before(sweep, it, rt))
                    a, b = bank_a[rt % 2], bank_b[rt % 2]
                    pe.wait_ge(s_evac, rows + 1)
                    if sweep != LAST:
                        nc.tensor.matmul(a[:, :], zeros[:, 0:P], zeros[:, :], start=True, stop=False,
                                         skip_group_check=True)
                    begun = []

                    def multiply(slot, uses, mt, off, paired):
                        pe.wait_ge(s_staged[slot], uses + 1)
                        pe.wait_ge(s_landed[slot], uses * 16 + 16)
                        for c in range(C):
                            if paired:
                                last = nc.tensor.matmul(a[:, :], staged_w[:, slot, c, :], ring_a[:, slot, c, :],
                                                        start=False, stop=False, skip_group_check=True)
                            else:
                                q = (c % 2) * F
                                last = nc.tensor.matmul(b[q:q + F, :], staged_w[:, slot, c, 0:F],
                                                        ring_a[:, slot, c, :], start=not begun and c < 2,
                                                        stop=False, skip_group_check=True)
                        begun.append(True)
                        last.then_inc(s_used[slot], 1)

                    def turn_previous():
                        if rt > 0:
                            turn_row(sweep, it, rt - 1)

                    def turn_vectors():
                        if sweep == 2:
                            pe.wait_ge(s_copied, it * M + rt + 1)
                            pe.wait_ge(s_read, rows + 1)
                            for c in range(C):
                                nc.tensor.transpose(turned_a[:, c, :], row_vectors[:, c, 0:2, :], ident[:, :])
                                last = nc.tensor.transpose(turned_b[:, c, :], row_vectors[:, c, 2:4, :], ident[:, :])
                            last.then_inc(s_vturned, 1)

                    blocks_of_row(pe, sweep, it, rt, ring, multiply, turn_previous, turn_vectors)
                    if sweep == 2:
                        pe.wait_ge(s_vready, it * M + rt + 1)
                        pe.wait_ge(s_final, rows)
                        if rt == 0:
                            pe.wait_ge(s_weights, 1)
                        for c in range(C):
                            nc.tensor.matmul(proj[rt % 2][:, c, 0:F], row_turned[:, 0, c * P:(c + 1) * P], w_ht1[:, :],
                                             start=(c == 0), stop=False, skip_group_check=True)
                            nc.tensor.matmul(proj[rt % 2][:, c, 0:F], row_turned[:, 1, c * P:(c + 1) * P],
                                             w_t2u3[:, :], start=False, stop=False, skip_group_check=True)
                    if sweep != LAST:
                        nc.tensor.matmul(a[:, 0:16], zeros[:, 0:P], zeros[:, 0:16], start=False, stop=True,
                                         skip_group_check=True)
                    nc.tensor.matmul(b[:, 0:16], zeros[:, 0:P], zeros[:, 0:16], start=False, stop=True,
                                     skip_group_check=True).then_inc(s_acc, 1)
                    if rt == M - 1:
                        turn_row(sweep, it, rt)
                macro_rows(pe, sweep, row)

        @block.scalar
        def _(act):
            for s in s_out:
                act.sem_inc(s, 16)
            for m in range(NM):
                n = CHUNKS // NM
                act.dma_start(resid[:, m * n:(m + 1) * n, :], x[:, m * n:(m + 1) * n, :]).then_inc(s_x[m], 16)
            w_rows = cheb_weight.rearrange("k i o -> (k i) o")
            loads = [(w_raw[:, 0, :], w_rows[0:2 * F, :]), (w_raw[:, 1, :], w_rows[2 * F:4 * F, :]),
                     (w_raw[0:F, 2, :], w_rows[3 * F:4 * F, :]), (w_raw[F:P, 2, :], w_rows[3 * F:4 * F, :]),
                     (w_raw[0:F, 3, :], hyp_kernel), (w_raw[F:P, 3, :], hyp_kernel),
                     (bias[:, 0, :], cheb_bias.partition_broadcast(P)),
                     (bias[:, 1, :], hyp_bias.partition_broadcast(P))]
            for dst, src in loads:
                act.dma_start(dst, src).then_inc(s_w, 16)

            with act.Fori(0, NB) as k:
                act.wait_ge(s_var, k + 1)
                nc.scalar.activation(small[:, 2, :], small[:, 1, :], ACT.Sqrt).then_inc(s_std, 1)

            with act.Fori(0, NM) as it:
                for rt in range(M):
                    t = act.snap(it * M + rt)
                    act.wait_ge(s_final, 2 * NB + 1)
                    act.wait_ge(s_vturned, t + 1)
                    nc.scalar.activation(row_vectors[:, :, :, :], nodes[:, bass.ds(t * C, C), :, :],
                                         ACT.Copy).then_inc(s_copied, 1)
                    act.wait_ge(s_var, t + NB + 1)
                    nc.scalar.activation(small[:, 2, :], small[:, 1, :], ACT.Sqrt).then_inc(s_std, 1)
                    act.wait_ge(s_square, t + 1)
                    nc.scalar.activation(small[:, 10, :], small[:, 7, :], ACT.Sqrt).then_inc(s_root, 1)
                    act.wait_ge(s_norm, t + 1)
                    nc.scalar.activation(small[:, 4, :], small[:, 3, :], ACT.Tanh).then_inc(s_func, 1)
            with act.Fori(0, NM) as it:
                for rt in range(M):
                    t = act.snap(it * M + rt)
                    act.wait_ge(s_square, t + NB + 1)
                    nc.scalar.activation(small[:, 10, :], small[:, 7, :], ACT.Sqrt).then_inc(s_root, 1)
                    act.wait_ge(s_norm, t + NB + 1)
                    nc.scalar.activation(small[:, 4, :], small[:, 3, :], ACT.Ln, bias=1.0, scale=1.0)
                    nc.scalar.activation(small[:, 5, :], small[:, 3, :], ACT.Ln, bias=1.0, scale=-1.0)\
                        .then_inc(s_func, 1)
                    act.wait_ge(s_result, t + 1)
                    row_at = act.snap((macro_of(LAST, it) * M + row_in_macro(LAST, rt)) * C)
                    act.dma_start(out[:, bass.ds(row_at, C), :], result[:, rt % 2, :, :]).then_inc(s_out[rt % 2], 16)
            for s in s_out:
                act.wait_ge(s, NB // 2 * 16 + 16)

        @block.vector
        def _(dve):
            def over_f(v):
                return v.unsqueeze(2).to_broadcast([P, C, F])

            def step(chain, ins):
                chain["n"] += 1
                ins.then_inc(s_chain, 1)
                dve.wait_ge(s_chain, chain["base"] + chain["n"])

            LN_STEPS = 5
            STEPS = [2, 3, LN_STEPS + 7, 20]
            starts = [NB * LN_STEPS + 2]
            for n in STEPS[:-1]:
                starts.append(starts[-1] + NB * n)

            def layernorm_relu(chain, v, dst, nth):
                total, var, std = small[:, 0, :], small[:, 1, :], small[:, 2, :]
                step(chain, nc.vector.tensor_reduce(total, v, AX.X, ALU.add))
                step(chain, nc.vector.scalar_tensor_tensor(tmp[:, 0], over_f(total), 1.0 / F, v, ALU.mult, ALU.subtract,
                                                           reverse1=True))
                step(chain, nc.vector.tensor_tensor(tmp[:, 1], tmp[:, 0], tmp[:, 0], ALU.mult))
                step(chain, nc.vector.tensor_reduce(var, tmp[:, 1], AX.X, ALU.add))
                nc.vector.tensor_scalar(var, var, 1.0 / F, LN_EPS, ALU.mult, ALU.add).then_inc(s_var, 1)
                dve.wait_ge(s_std, nth + 1)
                step(chain, nc.vector.reciprocal(total, std))
                return nc.vector.scalar_tensor_tensor(dst, tmp[:, 0], 0.0, over_f(total), ALU.max, ALU.mult)

            for s in (s_h, s_final, s_read):
                dve.sem_inc(s, 1)
            for m in range(NM):
                dve.wait_ge(s_x[m], 16)
                with dve.Fori(0, M) as k:
                    chain = {"n": 0, "base": dve.snap((k + m * M) * LN_STEPS)}
                    at = dve.snap((k + m * M) * C)
                    dve.wait_ge(s_h, k + m * M + 1)
                    layernorm_relu(chain, resid[:, bass.ds(at, C), :], nodes[:, bass.ds(at, C), H, :],
                                   k + m * M).then_inc(s_h, 1)

            dve.wait_ge(s_w, 8 * 16)
            chain = {"n": 0, "base": NB * LN_STEPS}
            nc.vector.tensor_copy(w_ht1[0:F, :], w_raw[0:F, 0, :])
            nc.vector.tensor_tensor(w_ht1[F:P, :], w_raw[F:P, 0, :], w_raw[F:P, 2, :], ALU.subtract)
            nc.vector.tensor_copy(w_t2u3[0:F, :], w_raw[0:F, 1, :])
            nc.vector.tensor_scalar(w_t2u3[F:P, :], w_raw[F:P, 1, :], 2.0, None, ALU.mult)
            nc.vector.tensor_scalar(w_u3u3[:, :], w_raw[:, 2, :], 2.0, None, ALU.mult)
            step(chain, nc.vector.memset(w_pair[:, :], 0.0))
            nc.vector.tensor_scalar(w_pair[0:F, 0:F], w_raw[0:F, 2, :], 2.0, None, ALU.mult)
            step(chain, nc.vector.tensor_copy(w_pair[F:P, F:2 * F], w_raw[F:P, 3, :]))
            nc.vector.memset(result[:, :, :, :], 0.0).then_inc(s_weights, 1)
            nc.vector.memset(acc_a[:, :], 0.0).then_inc(s_evac, 2)

            for sweep in range(SWEEPS):
                with dve.Fori(0, NM) as it:
                    chain = {"n": 0, "base": dve.snap(starts[sweep] + it * (M * STEPS[sweep]))}
                    for rt in range(M):
                        rows = dve.snap(done_before(sweep, it, rt))
                        at = dve.snap((macro_of(sweep, it) * M + row_in_macro(sweep, rt)) * C)
                        dve.compute_val(at)
                        own = [nodes[:, bass.ds(at, C), q, :] for q in range(4)]
                        own_resid = resid[:, bass.ds(at, C), :]
                        half = proj[rt % 2]

                        if sweep == 2:
                            dve.wait_ge(s_vturned, it * M + rt + 2)
                            nc.vector.tensor_copy(row_turned[:, 0, :], turned_a[:, :, :].rearrange("p c n -> p (c n)"))
                            nc.vector.tensor_copy(row_turned[:, 1, :], turned_b[:, :, :].rearrange("p c n -> p (c n)"))\
                                .then_inc(s_vready, 1)

                        dve.wait_ge(s_acc, rows + 1)
                        dve.wait_ge(s_turned, rows + 1)
                        if sweep != LAST:
                            nc.vector.tensor_copy(acc_a[:, :], bank_a[rt % 2][:, :])
                        nc.vector.tensor_copy(acc_b[:, :], bank_b[rt % 2][:, :]).then_inc(s_evac, 1)
                        dve.wait_ge(s_turned, rows + 2)
                        dve.wait_ge(s_final, rows + 1)

                        if sweep == 0:
                            step(chain, nc.vector.tensor_copy(tmp[:, 0], turned_b[:, :, 0:F]))
                            step(chain, nc.vector.tensor_tensor(tmp[:, 0], tmp[:, 0], turned_b[:, :, F:P], ALU.add))
                            nc.vector.tensor_tensor(own[T1], tmp[:, 0], turned_a[:, :, 0:F], ALU.add).then_inc(s_final, 1)
                            nc.vector.tensor_copy(own[T2], turned_a[:, :, F:P]).then_inc(s_read, 1)
                        if sweep == 1:
                            step(chain, nc.vector.tensor_tensor(tmp[:, 0], own[T2], turned_b[:, :, 0:F], ALU.add))
                            step(chain, nc.vector.tensor_tensor(tmp[:, 0], tmp[:, 0], turned_b[:, :, F:P], ALU.add))
                            step(chain, nc.vector.tensor_tensor(tmp[:, 0], tmp[:, 0], turned_a[:, :, 0:F], ALU.add))
                            nc.vector.tensor_copy(own[XP], turned_a[:, :, F:P]).then_inc(s_read, 1)
                            nc.vector.scalar_tensor_tensor(own[T2], tmp[:, 0], 2.0, own[H], ALU.mult, ALU.subtract)\
                                .then_inc(s_final, 1)
                        if sweep == 2:
                            step(chain, nc.vector.tensor_tensor(
                                tmp[:, 0], half[:, :, 0:F], bias[:, 0:1, :].to_broadcast([P, C, F]), ALU.add))
                            step(chain, nc.vector.tensor_tensor(own_resid, own_resid, tmp[:, 0], ALU.add))
                            nc.vector.tensor_copy(own[H], half[:, :, F:2 * F])
                            nc.vector.tensor_copy(own[T1], turned_a[:, :, F:P]).then_inc(s_read, 1)
                            step(chain, layernorm_relu(chain, own_resid, tmp[:, 2], NB + it * M + rt))
                            norm, func, ratio = small[:, 3, :], small[:, 4, :], small[:, 6, :]
                            step(chain, nc.vector.tensor_tensor(tmp[:, 1], tmp[:, 2], tmp[:, 2], ALU.mult))
                            nc.vector.tensor_reduce(small[:, 7, :], tmp[:, 1], AX.X, ALU.add).then_inc(s_square, 1)
                            dve.wait_ge(s_root, it * M + rt + 1)
                            nc.vector.tensor_scalar(norm, small[:, 10, :], MAX_NORM, None, ALU.min)\
                                .then_inc(s_norm, 1)
                            dve.wait_ge(s_norm, it * M + rt + 1)
                            step(chain, nc.vector.tensor_scalar(ratio, norm, EPS, None, ALU.add))
                            step(chain, nc.vector.reciprocal(small[:, 8, :], ratio))
                            dve.wait_ge(s_func, it * M + rt + 1)
                            step(chain, nc.vector.tensor_tensor(ratio, func, small[:, 8, :], ALU.mult))
                            nc.vector.tensor_tensor(own[XP], tmp[:, 2], over_f(ratio), ALU.mult).then_inc(s_final, 1)
                        if sweep == LAST:
                            radius, log_up, log_down = small[:, 3, :], small[:, 4, :], small[:, 5, :]
                            sq, series, mask, ratio = small[:, 6, :], small[:, 7, :], small[:, 8, :], small[:, 9, :]
                            step(chain, nc.vector.tensor_tensor(tmp[:, 0], own[T1], turned_b[:, :, 0:F], ALU.add))
                            nc.vector.tensor_tensor(tmp[:, 0], tmp[:, 0], turned_b[:, :, F:P], ALU.add).then_inc(s_read, 1)
                            dve.wait_ge(s_read, rows + 2)
                            step(chain, nc.vector.tensor_tensor(tmp[:, 1], tmp[:, 0], tmp[:, 0], ALU.mult))
                            nc.vector.tensor_reduce(small[:, 7, :], tmp[:, 1], AX.X, ALU.add).then_inc(s_square, 1)
                            dve.wait_ge(s_root, NB + it * M + rt + 1)
                            nc.vector.tensor_scalar(radius, small[:, 10, :], MAX_RADIUS, None, ALU.min)\
                                .then_inc(s_norm, 1)
                            dve.wait_ge(s_norm, NB + it * M + rt + 1)
                            step(chain, nc.vector.tensor_tensor(sq, radius, radius, ALU.mult))
                            step(chain, nc.vector.tensor_scalar(series, sq, 1.0 / 13, None, ALU.mult))
                            for k in (11, 9, 7, 5, 3):
                                step(chain, nc.vector.scalar_tensor_tensor(series, series, 1.0 / k, sq, ALU.add, ALU.mult))
                            step(chain, nc.vector.scalar_tensor_tensor(series, series, 1.0, radius, ALU.add, ALU.mult))
                            nc.vector.tensor_scalar(mask, radius, SERIES_BELOW, None, ALU.is_ge)
                            step(chain, nc.vector.tensor_tensor(tmp[:, 2], own[H], half[:, :, 0:F], ALU.add))
                            dve.wait_ge(s_func, NB + it * M + rt + 1)
                            step(chain, nc.vector.tensor_tensor(ratio, log_up, log_down, ALU.subtract))
                            step(chain, nc.vector.scalar_tensor_tensor(ratio, ratio, 0.5, series, ALU.mult, ALU.subtract))
                            step(chain, nc.vector.tensor_tensor(ratio, ratio, mask, ALU.mult))
                            step(chain, nc.vector.tensor_tensor(ratio, ratio, series, ALU.add))
                            step(chain, nc.vector.tensor_scalar(small[:, 11, :], radius, EPS, None, ALU.add))
                            step(chain, nc.vector.reciprocal(small[:, 10, :], small[:, 11, :]))
                            step(chain, nc.vector.tensor_tensor(ratio, ratio, small[:, 10, :], ALU.mult))
                            step(chain, nc.vector.tensor_tensor(tmp[:, 1], tmp[:, 2], over_f(ratio), ALU.mult))
                            step(chain, nc.vector.tensor_tensor(
                                tmp[:, 2], tmp[:, 1], bias[:, 1:2, :].to_broadcast([P, C, F]), ALU.add))
                            dve.wait_ge(s_out[rt % 2], it * (M // 2 * 16) + rt // 2 * 16 + 16)
                            nc.vector.tensor_tensor(result[:, rt % 2], tmp[:, 2], own_resid, ALU.add).then_inc(s_result, 1)
                            dve.wait_ge(s_result, it * M + rt + 1)
                            nc.vector.memset(small[:, 0, 0:1], 0.0).then_inc(s_final, 1)
                    assert chain["n"] == M * STEPS[sweep], (sweep, chain["n"])


def kernel(x, adj, L0_gnn_weight, L0_gnn_bias, L1_gnn_kernel, L1_gnn_bias):
    import numpy as np
    import concourse.bacc as bacc
    from concourse.bass_utils import run_bass_kernel_spmd

    n, f = x.shape
    p, c = 128, 4
    b = p * c
    x_laid = np.ascontiguousarray(np.asarray(x).reshape(n // p, p, f).transpose(1, 0, 2))
    adj_laid = np.ascontiguousarray(np.asarray(adj).reshape(n // b, b, n // b, c, p).transpose(0, 2, 4, 3, 1))\
        .reshape((n // b) ** 2 * p, c, b)
    arrays = {"x": x_laid, "adj_blocks": adj_laid, "cheb_weight": np.ascontiguousarray(L0_gnn_weight),
              "cheb_bias": np.ascontiguousarray(L0_gnn_bias), "hyp_kernel": np.ascontiguousarray(L1_gnn_kernel),
              "hyp_bias": np.ascontiguousarray(L1_gnn_bias)}
    nc = bacc.Bacc("TRN2", target_bir_lowering=False, num_devices=1)
    args = [nc.dram_tensor(k, a.shape, mybir.dt.from_np(a.dtype), kind="ExternalInput").ap() for k, a in arrays.items()]
    args.append(nc.dram_tensor("out", x_laid.shape, mybir.dt.float32, kind="ExternalOutput").ap())
    chebyshev_hyperbolic_kernel(nc, *args)
    r = run_bass_kernel_spmd(nc, [arrays], core_ids=[0])
    got = r.results[0]["out"]
    return np.ascontiguousarray(got.transpose(1, 0, 2)).reshape(n, f)
```

```python
import concourse.bass as bass
from concourse import mybir
from contextlib import ExitStack


def chebyshev_hyperbolic_kernel(nc, x, adj_blocks, cheb_weight, cheb_bias, hyp_kernel, hyp_bias, out):
    fp32 = mybir.dt.float32
    bf16 = mybir.dt.bfloat16
    ALU = mybir.AluOpType
    ACT = mybir.ActivationFunctionType
    AX = mybir.AxisListType

    P = 128
    F = x.shape[2]
    CHUNKS = x.shape[1]
    C = 4
    BLOCK = C * P
    NB = CHUNKS // C
    M = 4
    NM = NB // M
    SWEEPS = 4
    LAST = SWEEPS - 1
    LN_EPS = 1e-5
    EPS = 1e-8
    MAX_NORM = 10.0
    MAX_RADIUS = 0.999
    SERIES_BELOW = 0.25

    H, T1, T2, XP = range(4)
    LEFT = [H, T1, T2, XP]
    SINGLE, PAIR, LATE = range(3)

    DOWN = [True, False, True, True]

    def macro_of(sweep, it):
        return it if DOWN[sweep] else NM - 1 - it

    def row_in_macro(sweep, rt):
        return rt if DOWN[sweep] else M - 1 - rt

    def row_index(sweep, it, rt):
        if sweep == LAST:
            return (NM - 1 - rt) * M + it
        return macro_of(sweep, it) * M + row_in_macro(sweep, rt)

    def near_before_far(sweep, rt):
        r = row_in_macro(sweep, rt)
        if sweep == 0:
            return [(r, j, SINGLE) for j in range(r, M)]
        return [(r, r, SINGLE)]

    def near_after_far(sweep, rt):
        r = row_in_macro(sweep, rt)
        columns = range(M - 1, r, -1) if sweep == 1 else range(r)
        return [(r, j, PAIR) for j in columns]

    def closing(sweep):
        if sweep != 2:
            return []
        return [(k, j, LATE) for j in range(M - 1) for k in range(j + 1)] + \
            [(k, M - 1, LATE) for k in reversed(range(M))]

    def far_parts(sweep, it):
        if sweep == 0:
            return [(it, lambda g: g, PAIR), (NM - 1 - it, lambda g: it + 1 + g, SINGLE)]
        return [(it, lambda g: g, PAIR)]

    def uses_before(sweep, it, slot):
        def near(sweep):
            n = len(closing(sweep)) + sum(len(near_before_far(sweep, r)) + len(near_after_far(sweep, r))
                                          for r in range(M))
            return -(-(n - slot) // M)

        if sweep == 0:
            return it * (near(0) + M * (NM - 1))
        start = NM * (NM * M)
        for before in range(1, sweep):
            start = start + NM * near(before) + M * NM * (NM - 1) // 2
        if sweep == LAST:
            return start + it * (NM * (NM - 1) // 2)
        return start + it * (near(sweep) - M // 2) + it * it * (M // 2)

    def visitor(e, ring, block):
        def visit(position, groups, macro_row, place, mt, col, kind):
            slot = position % M
            uses = e.snap(ring["before"][slot] + groups + position // M)
            e.compute_val(uses + 1)
            block(slot, uses, macro_row, place, mt, col, kind)
        return visit

    def blocks_of_row(e, sweep, it, rt, ring, block, after_first, after_far):
        visit = visitor(e, ring, block)

        def far(count, nth, groups, macro_row, place, kind):
            with e.Fori(0, count) as g:
                mt = nc.s_assert_within(nth(g), 0, NM - 1, skip_runtime_bounds_check_because=
                                        "the far columns end at the last macro column")
                for k in range(M):
                    visit(ring["position"] + k, groups + g, macro_row, place, mt,
                          k if DOWN[sweep] else M - 1 - k, kind)

        def near(parts, groups):
            for place, col, kind in parts:
                visit(ring["position"], groups, macro_of(sweep, it), place, it, col, kind)
                ring["position"] += 1

        if sweep == LAST:
            groups = rt * (rt - 1) // 2
            if rt > 0:
                far(1, lambda g: g + (NM - rt), groups, NM - 1 - rt, it, SINGLE)
            after_first()
            if rt > 1:
                far(rt - 1, lambda g: g + (NM - rt + 1), groups + 1, NM - 1 - rt, it, SINGLE)
            return
        in_row = NM - 1 if sweep == 0 else it
        groups = in_row * rt
        first = near_before_far(sweep, rt)
        near(first[:1], groups)
        after_first()
        near(first[1:], groups)
        done = groups
        for count, nth, kind in far_parts(sweep, it):
            with e.If(count > 0):
                far(count, nth, done, macro_of(sweep, it), row_in_macro(sweep, rt), kind)
            done = done + it
        after_far()
        near(near_after_far(sweep, rt), groups + in_row)

    def closing_blocks(e, sweep, it, ring, block, after_first):
        visit = visitor(e, ring, block)
        for n, (place, col, kind) in enumerate(closing(sweep)):
            visit(ring["position"], it * M, macro_of(sweep, it), place, it, col, kind)
            ring["position"] += 1
            if n == 0:
                after_first()

    def iterations(e, sweep, row, close):
        with e.Fori(0, NM) as it:
            ring = {"position": 0, "before": [e.snap(uses_before(sweep, it, s)) for s in range(M)]}
            for rt in range(M):
                row(it, rt, ring)
            if closing(sweep):
                close(it, ring)

    def nothing():
        pass

    ctx = ExitStack()
    with ctx:
        def sb(name, shape, dt=fp32):
            return ctx.enter_context(nc.sbuf_tensor(name, shape, dt))

        def pb(name, shape):
            return ctx.enter_context(nc.psum_tensor(name, shape, fp32))

        def sem(name):
            return ctx.enter_context(nc.semaphore(name))

        nodes = sb("nodes", [P, CHUNKS, 4, F])
        resid = sb("resid", [P, CHUNKS, F])
        ring_a = sb("ring_a", [P, M, C, BLOCK])
        staged_w = sb("staged_w", [P, M, C, 2 * F])
        partial = sb("partial", [P, NB, BLOCK])
        acc = sb("acc", [P, BLOCK])
        h_turned = sb("h_turned", [F, BLOCK])
        ident = sb("ident", [P, P])
        zeros = sb("zeros", [P, BLOCK], bf16)
        w_raw = sb("w_raw", [P, 5, F])
        w_term = sb("w_term", [P, 4, F])
        bias = sb("bias", [P, 2, F])
        tmp = sb("tmp", [P, 4, C, F])
        squares = sb("squares", [P, 2, C])
        roots = sb("roots", [P, 2, C])
        small = sb("small", [P, 12, C])
        result = sb("result", [P, 2, C, F])

        bank_a = [pb(f"bank_a{i}", [P, BLOCK]) for i in range(2)]
        bank_b = [pb(f"bank_b{i}", [P, BLOCK]) for i in range(2)]
        turned = pb("turned", [P, C, P])
        h_bank = pb("h_bank", [P, BLOCK])
        late_banks = [h_bank[:, :], turned[:, :, :].rearrange("p c n -> p (c n)"), bank_a[0][:, :], bank_b[0][:, :]]
        HIGH, LOW = (2, 3), (0, 1)
        proj = [pb(f"proj{i}", [P, C, F]) for i in range(2)]

        s_x = [sem(f"x_landed{i}") for i in range(NM)]
        s_w = sem("weights_landed")
        s_ident0 = sem("ident_zeroed")
        s_const = sem("constants_ready")
        s_weights = sem("weights_ready")
        s_landed = [sem(f"block_landed{i}") for i in range(M)]
        s_staged = [sem(f"weights_staged{i}") for i in range(M)]
        s_used = [sem(f"slot_used{i}") for i in range(M)]
        s_h = sem("h_ready")
        s_acc = sem("row_accumulated")
        s_evac = sem("row_evacuated")
        s_kept = sem("row_kept")
        s_turned = sem("row_turned_back")
        s_read = sem("turned_read")
        s_final = sem("row_final")
        s_hturned = sem("h_turned")
        s_hready = sem("h_turned_ready")
        s_late = sem("late_accumulated")
        s_high = sem("late_high_added")
        s_low = sem("late_low_added")
        s_var = sem("variance_ready")
        s_std = sem("deviation_ready")
        s_square = sem("norm_squared_ready")
        s_root = sem("norm_root_ready")
        s_norm = sem("norm_ready")
        s_func = sem("function_ready")
        s_chain = sem("vector_chain")
        s_result = sem("result_ready")
        s_out = [sem(f"result_stored{i}") for i in range(2)]

        block = ctx.enter_context(nc.Block())

        def done_before(sweep, it, rt):
            return sweep * NB + it * M + rt

        def order(sweep, mt, off):
            return mt * M + (off if DOWN[sweep] else M - 1 - off) + 1

        @block.sync
        def _(sp):
            for sweep in range(SWEEPS):
                def load(slot, uses, macro_row, place, mt, col, kind):
                    at = sp.snap(((macro_row * M + place) * NB + macro_of(sweep, mt) * M + col) * P)
                    sp.compute_val(at)
                    sp.wait_ge(s_const, 1)
                    sp.wait_ge(s_used[slot], uses + 1)
                    sp.dma_start(ring_a[:, slot, :, :], adj_blocks[bass.ds(at, P), :, :])\
                        .then_inc(s_landed[slot], 16)

                iterations(sp, sweep,
                           lambda it, rt, ring: blocks_of_row(sp, sweep, it, rt, ring, load, nothing, nothing),
                           lambda it, ring: closing_blocks(sp, sweep, it, ring, load, nothing))

        @block.gpsimd
        def _(pool):
            nc.gpsimd.memset(zeros[:, :], 0.0)
            nc.gpsimd.memset(ident[:, :], 0.0).then_inc(s_ident0, 1)
            pool.wait_ge(s_ident0, 1)
            nc.gpsimd.affine_select(out=ident[:, :], in_=ident[:, :], compare_op=ALU.not_equal, fill=1.0,
                                    base=0, pattern=[[-1, P]], channel_multiplier=1).then_inc(s_const, 1)

            for sweep in range(SWEEPS):
                def stage(slot, uses, macro_row, place, mt, col, kind):
                    J = pool.snap(macro_of(sweep, mt) * M + col)
                    left = XP if kind == LATE else LEFT[sweep]
                    width = 2 if kind == PAIR else 1
                    if sweep == 0 and kind == SINGLE:
                        known, count = s_h, order(sweep, mt, col) + 1
                    elif kind == SINGLE:
                        known, count = s_final, sweep * NB + 1
                    else:
                        known, count = s_final, sweep * NB + order(sweep, mt, col) + 1
                    pool.compute_val(count)
                    pool.wait_ge(s_const, 1)
                    pool.wait_ge(known, count)
                    pool.wait_ge(s_used[slot], uses + 1)
                    nc.gpsimd.tensor_copy(
                        staged_w[:, slot, :, 0:width * F].rearrange("p c (w f) -> p c w f", w=width),
                        nodes[:, bass.ds(J * C, C), left:left + width, :]).then_inc(s_staged[slot], 1)

                iterations(pool, sweep,
                           lambda it, rt, ring: blocks_of_row(pool, sweep, it, rt, ring, stage, nothing, nothing),
                           lambda it, ring: closing_blocks(pool, sweep, it, ring, stage, nothing))

        @block.tensor
        def _(pe):
            for s in s_used + [s_turned, s_high]:
                pe.sem_inc(s, 1)
            pe.wait_ge(s_const, 1)

            def turn_row(sweep, it, rt):
                rows = pe.snap(done_before(sweep, it, rt))
                weight = w_raw[:, 4, :] if sweep == LAST else w_term[:, sweep + 1, :]
                pe.wait_ge(s_evac, rows + 3)
                if sweep != 2:
                    pe.wait_ge(s_read, rows + 2)
                    for c in range(C):
                        nc.tensor.transpose(turned[:, c, :], acc[:, c * P:(c + 1) * P], ident[:, :])
                if sweep != 0:
                    pe.wait_ge(s_read, rows + 1)
                for c in range(C):
                    last = nc.tensor.matmul(proj[rt % 2][:, c, :], acc[:, c * P:(c + 1) * P], weight,
                                            start=(sweep != 0 and c == 0), stop=True, skip_group_check=True)
                last.then_inc(s_turned, 1)

            def multiply_late(it, slot, uses, place, col):
                if place == col:
                    if place in LOW:
                        pe.wait_ge(s_low, it + 1)
                        pe.wait_ge(s_read, 2 * NB + 2)
                    else:
                        rows = done_before(2, it, 2)
                        pe.wait_ge(s_evac, rows + 3)
                        pe.wait_ge(s_kept, rows + 3)
                pe.wait_ge(s_staged[slot], uses + 1)
                pe.wait_ge(s_landed[slot], uses * 16 + 16)
                for c in range(C):
                    q = (c % 2) * F
                    last = nc.tensor.matmul(late_banks[place][q:q + F, :], staged_w[:, slot, c, 0:F],
                                            ring_a[:, slot, c, :], start=place == col and c < 2, stop=False,
                                            skip_group_check=True)
                last.then_inc(s_used[slot], 1)
                if (place, col) in ((HIGH[0], M - 1), (LOW[0], M - 1)):
                    for k in HIGH if place in HIGH else LOW:
                        last = nc.tensor.matmul(late_banks[k][:, 0:16], zeros[:, 0:P], zeros[:, 0:16],
                                                start=False, stop=True, skip_group_check=True)
                    last.then_inc(s_late, 1)

            for sweep in range(SWEEPS):
                def row(it, rt, ring):
                    rows = pe.snap(done_before(sweep, it, rt))
                    a, b = bank_a[rt % 2], bank_b[rt % 2]
                    pe.wait_ge(s_evac, rows + 1)
                    if sweep != LAST:
                        pe.wait_ge(s_kept, rows + 1)
                    if sweep == 2 and rt == 0:
                        pe.wait_ge(s_high, it + 1)
                    if sweep == LAST and rt < 2:
                        pe.wait_ge(s_high, NM + 1)
                        pe.wait_ge(s_low, NM + 1)
                    whole = a if sweep != LAST else b
                    nc.tensor.matmul(whole[:, :], zeros[:, 0:P], zeros[:, :], start=True, stop=False,
                                     skip_group_check=True)
                    begun = []

                    def multiply(slot, uses, macro_row, place, mt, col, kind):
                        if kind == LATE:
                            multiply_late(it, slot, uses, place, col)
                            return
                        if sweep == 0 and not begun:
                            pe.compute_val(rows + 1)
                            pe.wait_ge(s_const, 1)
                        pe.wait_ge(s_staged[slot], uses + 1)
                        if sweep == 0 and not begun:
                            pe.wait_ge(s_hready, rows + 1)
                            for c in range(C):
                                last = nc.tensor.transpose(h_bank[0:F, c * P:(c + 1) * P],
                                                           staged_w[:, slot, c, 0:F], ident[:, :])
                            last.then_inc(s_hturned, 1)
                        pe.wait_ge(s_landed[slot], uses * 16 + 16)
                        for c in range(C):
                            if kind == PAIR:
                                last = nc.tensor.matmul(a[:, :], staged_w[:, slot, c, :], ring_a[:, slot, c, :],
                                                        start=False, stop=False, skip_group_check=True)
                            else:
                                q = (c % 2) * F
                                last = nc.tensor.matmul(b[q:q + F, :], staged_w[:, slot, c, 0:F],
                                                        ring_a[:, slot, c, :],
                                                        start=sweep != LAST and not begun and c < 2,
                                                        stop=False, skip_group_check=True)
                        begun.append(True)
                        last.then_inc(s_used[slot], 1)

                    def turn_previous():
                        if rt > 0:
                            turn_row(sweep, it, rt - 1)

                    def project_h():
                        if sweep == 0:
                            pe.wait_ge(s_hready, rows + 2)
                            pe.wait_ge(s_weights, 1)
                            pe.wait_ge(s_read, rows + 1)
                            for c in range(C):
                                nc.tensor.matmul(proj[rt % 2][:, c, :], h_turned[:, c * P:(c + 1) * P],
                                                 w_term[0:F, 0, :], start=(c == 0), stop=False, skip_group_check=True)

                    blocks_of_row(pe, sweep, it, rt, ring, multiply, turn_previous, project_h)
                    if sweep != LAST:
                        nc.tensor.matmul(a[:, 0:16], zeros[:, 0:P], zeros[:, 0:16], start=False, stop=True,
                                         skip_group_check=True)
                    nc.tensor.matmul(b[:, 0:16], zeros[:, 0:P], zeros[:, 0:16], start=False, stop=True,
                                     skip_group_check=True).then_inc(s_acc, 1)
                    if rt == M - 1 and not closing(sweep):
                        turn_row(sweep, it, rt)

                def close(it, ring):
                    def late(slot, uses, macro_row, place, mt, col, kind):
                        multiply_late(it, slot, uses, place, col)
                    closing_blocks(pe, sweep, it, ring, late, lambda: turn_row(sweep, it, M - 1))

                iterations(pe, sweep, row, close)

        @block.scalar
        def _(act):
            for s in s_out:
                act.sem_inc(s, 16)
            for m in range(NM):
                n = CHUNKS // NM
                act.dma_start(resid[:, m * n:(m + 1) * n, :], x[:, m * n:(m + 1) * n, :]).then_inc(s_x[m], 16)
            loads = [(bias[:, 0, :], cheb_bias.partition_broadcast(P)), (bias[:, 1, :], hyp_bias.partition_broadcast(P))]
            for part in (slice(0, F), slice(F, P)):
                loads += [(w_raw[part, 0:4, :], cheb_weight.rearrange("k i o -> i k o")), (w_raw[part, 4, :], hyp_kernel)]
            for dst, src in loads:
                act.dma_start(dst, src).then_inc(s_w, 16)

            with act.Fori(0, NB // 2) as k:
                act.wait_ge(s_var, k + 1)
                nc.scalar.activation(roots[:, :, :], squares[:, :, :], ACT.Sqrt).then_inc(s_std, 1)

            def keep(sweep, it, rt):
                i = act.snap(row_index(sweep, it, rt))
                act.wait_ge(s_evac, done_before(sweep, it, rt) + 3)
                nc.scalar.activation(partial[F:P, bass.ds(i, 1), :], bank_a[rt % 2][F:P, :].unsqueeze(1),
                                     ACT.Copy).then_inc(s_kept, 1)

            for sweep in (0, 1):
                with act.Fori(0, NM) as it:
                    for rt in range(M):
                        keep(sweep, it, rt)
            with act.Fori(0, NM) as it:
                for rt in range(M):
                    t = act.snap(it * M + rt)
                    keep(2, it, rt)
                    act.wait_ge(s_var, t + (NB // 2 + 1))
                    nc.scalar.activation(roots[:, :, :], squares[:, :, :], ACT.Sqrt).then_inc(s_std, 1)
                    act.wait_ge(s_norm, t + 1)
                    nc.scalar.activation(small[:, 4, :], small[:, 3, :], ACT.Tanh).then_inc(s_func, 1)
                    nc.scalar.activation(small[:, 5, :], ident[:, 0:C], ACT.Sqrt)
            with act.Fori(0, NM) as it:
                for rt in range(M):
                    t = act.snap(it * M + rt)
                    act.wait_ge(s_square, t + 1)
                    nc.scalar.activation(small[:, 10, :], small[:, 7, :], ACT.Sqrt).then_inc(s_root, 1)
                    act.wait_ge(s_norm, t + NB + 1)
                    nc.scalar.activation(small[:, 4, :], small[:, 3, :], ACT.Ln, bias=1.0, scale=1.0)
                    nc.scalar.activation(small[:, 5, :], small[:, 3, :], ACT.Ln, bias=1.0, scale=-1.0)\
                        .then_inc(s_func, 1)
                    act.wait_ge(s_result, t + 1)
                    row_at = act.snap(row_index(LAST, it, rt) * C)
                    act.dma_start(out[:, bass.ds(row_at, C), :], result[:, rt % 2, :, :]).then_inc(s_out[rt % 2], 16)
            for s in s_out:
                act.wait_ge(s, NB // 2 * 16 + 16)

        @block.vector
        def _(dve):
            def over_f(v):
                return v.unsqueeze(2).to_broadcast([P, C, F])

            def step(chain, ins):
                chain["n"] += 1
                ins.then_inc(s_chain, 1)
                dve.wait_ge(s_chain, chain["base"] + chain["n"])

            LN_STEPS = 5
            LN_STEPS = 5
            STEPS = [3, 3, 11, 19]
            starts = [NB // 2 * LN_STEPS]
            for n in STEPS[:-1]:
                starts.append(starts[-1] + NB * n)

            def centred(chain, v, dst, total):
                step(chain, nc.vector.tensor_reduce(total, v, AX.X, ALU.add))
                return nc.vector.scalar_tensor_tensor(
                    dst, total.unsqueeze(2).to_broadcast(list(v.shape)), 1.0 / F, v, ALU.mult, ALU.subtract, reverse1=True)

            for s in (s_h, s_final, s_hready):
                dve.sem_inc(s, 1)
            for s in (s_evac, s_kept, s_read):
                dve.sem_inc(s, 2)
            pair, pair_sq = (tmp[:, k:k + 2].rearrange("p k c f -> p (k c) f") for k in (0, 2))
            square_sums, std = (v[:, :, :].rearrange("p k c -> p (k c)") for v in (squares, roots))
            for m in range(NM):
                dve.wait_ge(s_x[m], 16)
                with dve.Fori(0, M // 2) as k:
                    nth = dve.snap(k + m * (M // 2))
                    chain = {"n": 0, "base": dve.snap(nth * LN_STEPS)}
                    at = dve.snap(nth * (2 * C))
                    dve.wait_ge(s_h, nth * 2 + 1)
                    step(chain, centred(chain, resid[:, bass.ds(at, 2 * C), :], pair, small[:, 0:2, :].rearrange("p k c -> p (k c)")))
                    step(chain, nc.vector.tensor_tensor(pair_sq, pair, pair, ALU.mult))
                    step(chain, nc.vector.tensor_reduce(square_sums, pair_sq, AX.X, ALU.add))
                    nc.vector.tensor_scalar(square_sums, square_sums, 1.0 / F, LN_EPS, ALU.mult, ALU.add).then_inc(s_var, 1)
                    dve.wait_ge(s_std, nth + 1)
                    rstd = small[:, 0:2, :].rearrange("p k c -> p (k c)")
                    step(chain, nc.vector.reciprocal(rstd, std))
                    nc.vector.scalar_tensor_tensor(nodes[:, bass.ds(at, 2 * C), H, :], pair, 0.0,
                                                   rstd.unsqueeze(2).to_broadcast([P, 2 * C, F]), ALU.max, ALU.mult)\
                        .then_inc(s_h, 2)
                if m == 0:
                    dve.wait_ge(s_w, 6 * 16)
                    nc.vector.tensor_tensor(w_term[:, 0:2, :], w_raw[:, 0:2, :], w_raw[:, 2:4, :], ALU.subtract)
                    nc.vector.tensor_scalar(w_term[:, 2:4, :], w_raw[:, 2:4, :], 2.0, None, ALU.mult).then_inc(s_weights, 1)

            nc.vector.memset(partial[0:F, :, :], 0.0).then_inc(s_low, 1)

            for sweep in range(SWEEPS):
                with dve.Fori(0, NM) as it:
                    chain = {"n": 0, "base": dve.snap(starts[sweep] + it * (M * STEPS[sweep]))}
                    for rt in range(M):
                        rows = dve.snap(done_before(sweep, it, rt))
                        at = dve.snap(row_index(sweep, it, rt) * C)
                        dve.compute_val(at)
                        own = [nodes[:, bass.ds(at, C), q, :] for q in range(4)]
                        own_resid = resid[:, bass.ds(at, C), :]
                        half = proj[rt % 2]

                        i = dve.snap(row_index(sweep, it, rt))
                        dve.compute_val(i)

                        if sweep == 0:
                            dve.wait_ge(s_hturned, rows + 1)
                            nc.vector.tensor_copy(h_turned[:, :], h_bank[0:F, :]).then_inc(s_hready, 1)

                        dve.wait_ge(s_acc, rows + 1)
                        dve.wait_ge(s_turned, rows + 1)
                        if sweep != 0:
                            dve.wait_ge(s_kept, sweep * NB + 2)
                        bank = bank_b[rt % 2]
                        if sweep == LAST:
                            dve.wait_ge(s_high, NM + 1)
                            dve.wait_ge(s_low, NM + 1)
                        own_part = partial[:, bass.ds(i, 1), :]
                        if sweep == 0:
                            step(chain, nc.vector.tensor_copy(acc[:, :], bank[:, :]))
                        elif sweep == LAST:
                            nc.vector.tensor_tensor(acc[:, :].unsqueeze(1), own_part, bank[:, :].unsqueeze(1),
                                                    ALU.add).then_inc(s_evac, 1)
                        else:
                            nc.vector.tensor_copy(acc[0:F, :], bank[0:F, :])
                            step(chain, nc.vector.tensor_tensor(acc[F:P, :].unsqueeze(1), own_part[F:P],
                                                                bank[F:P, :].unsqueeze(1), ALU.add))
                        if sweep != LAST:
                            nc.vector.tensor_tensor(acc[0:F, :], acc[0:F, :], bank_a[rt % 2][0:F, :], ALU.add)\
                                .then_inc(s_evac, 1)
                        dve.wait_ge(s_turned, rows + 2)
                        dve.wait_ge(s_final, rows + 1)
                        dve.wait_ge(s_read, rows + 2)
                        sums = turned[:, :, 0:F], turned[:, :, F:P]

                        if sweep != 2:
                            step(chain, nc.vector.tensor_copy(tmp[:, 1], sums[0]))
                        if sweep == 0:
                            nc.vector.tensor_tensor(own[T1], tmp[:, 1], sums[1], ALU.add).then_inc(s_final, 1)
                            step(chain, nc.vector.tensor_tensor(
                                tmp[:, 0], half[:, :, :], bias[:, 0:1, :].to_broadcast([P, C, F]), ALU.add))
                            nc.vector.tensor_tensor(own_resid, own_resid, tmp[:, 0], ALU.add).then_inc(s_read, 1)
                        if sweep == 1:
                            step(chain, nc.vector.tensor_tensor(tmp[:, 0], tmp[:, 1], sums[1], ALU.add))
                            nc.vector.scalar_tensor_tensor(own[T2], tmp[:, 0], 2.0, own[H], ALU.mult, ALU.subtract)\
                                .then_inc(s_final, 1)
                            nc.vector.tensor_tensor(own_resid, own_resid, half[:, :, :], ALU.add).then_inc(s_read, 1)
                        if sweep == 2:
                            nc.vector.tensor_tensor(own_resid, own_resid, half[:, :, :], ALU.add).then_inc(s_read, 1)
                            dve.compute_val(rows + 3)
                            dve.wait_ge(s_const, 1)
                            dve.wait_ge(s_read, rows + 3)
                            v = tmp[:, 2]
                            step(chain, centred(chain, own_resid, v, small[:, 0, :]))
                            nc.vector.tensor_tensor(tmp[:, 0], v, v, ALU.mult)
                            step(chain, nc.vector.scalar_tensor_tensor(tmp[:, 1], v, 0.0, v, ALU.max, ALU.mult))
                            step(chain, nc.vector.tensor_reduce(square_sums, tmp[:, 0:2].rearrange("p k c f -> p (k c) f"),
                                                                AX.X, ALU.add))
                            nc.vector.tensor_scalar(squares[:, 0, :], squares[:, 0, :], 1.0 / F, LN_EPS,
                                                    ALU.mult, ALU.add).then_inc(s_var, 1)
                            dve.wait_ge(s_std, it * M + (rt + NB // 2 + 1))
                            norm, func, rstd, ratio = small[:, 3, :], small[:, 4, :], small[:, 1, :], small[:, 6, :]
                            step(chain, nc.vector.reciprocal(rstd, roots[:, 0, :]))
                            step(chain, nc.vector.tensor_tensor(ratio, roots[:, 1, :], rstd, ALU.mult))
                            nc.vector.tensor_scalar(norm, ratio, MAX_NORM, None, ALU.min).then_inc(s_norm, 1)
                            dve.wait_ge(s_norm, it * M + rt + 1)
                            step(chain, nc.vector.tensor_scalar(small[:, 7, :], norm, EPS, None, ALU.add))
                            step(chain, nc.vector.reciprocal(small[:, 8, :], small[:, 7, :]))
                            step(chain, nc.vector.tensor_tensor(ratio, small[:, 8, :], rstd, ALU.mult))
                            dve.wait_ge(s_func, it * M + rt + 1)
                            step(chain, nc.vector.tensor_tensor(small[:, 9, :], func, ratio, ALU.mult))
                            nc.vector.scalar_tensor_tensor(own[XP], v, 0.0, over_f(small[:, 9, :]), ALU.max, ALU.mult)\
                                .then_inc(s_final, 1)
                        if sweep == LAST:
                            radius, log_up, log_down = small[:, 3, :], small[:, 4, :], small[:, 5, :]
                            sq, series, mask, ratio = small[:, 6, :], small[:, 7, :], small[:, 8, :], small[:, 9, :]
                            step(chain, nc.vector.tensor_tensor(tmp[:, 0], tmp[:, 1], sums[1], ALU.add))
                            step(chain, nc.vector.tensor_tensor(tmp[:, 1], tmp[:, 0], tmp[:, 0], ALU.mult))
                            nc.vector.tensor_reduce(small[:, 7, :], tmp[:, 1], AX.X, ALU.add).then_inc(s_square, 1)
                            dve.wait_ge(s_root, it * M + rt + 1)
                            nc.vector.tensor_scalar(radius, small[:, 10, :], MAX_RADIUS, None, ALU.min)\
                                .then_inc(s_norm, 1)
                            dve.wait_ge(s_norm, NB + it * M + rt + 1)
                            step(chain, nc.vector.tensor_tensor(sq, radius, radius, ALU.mult))
                            step(chain, nc.vector.tensor_scalar(series, sq, 1.0 / 13, None, ALU.mult))
                            for k in (11, 9, 7, 5, 3):
                                step(chain, nc.vector.scalar_tensor_tensor(series, series, 1.0 / k, sq, ALU.add, ALU.mult))
                            step(chain, nc.vector.scalar_tensor_tensor(series, series, 1.0, radius, ALU.add, ALU.mult))
                            nc.vector.tensor_scalar(mask, radius, SERIES_BELOW, None, ALU.is_ge)
                            dve.wait_ge(s_func, NB + it * M + rt + 1)
                            step(chain, nc.vector.tensor_tensor(ratio, log_up, log_down, ALU.subtract))
                            step(chain, nc.vector.scalar_tensor_tensor(ratio, ratio, 0.5, series, ALU.mult, ALU.subtract))
                            step(chain, nc.vector.tensor_tensor(ratio, ratio, mask, ALU.mult))
                            step(chain, nc.vector.tensor_tensor(ratio, ratio, series, ALU.add))
                            step(chain, nc.vector.tensor_scalar(small[:, 11, :], radius, EPS, None, ALU.add))
                            step(chain, nc.vector.reciprocal(small[:, 10, :], small[:, 11, :]))
                            step(chain, nc.vector.tensor_tensor(ratio, ratio, small[:, 10, :], ALU.mult))
                            nc.vector.tensor_tensor(tmp[:, 2], half[:, :, :], over_f(ratio), ALU.mult).then_inc(s_read, 1)
                            dve.wait_ge(s_read, rows + 3)
                            step(chain, nc.vector.tensor_tensor(
                                tmp[:, 1], tmp[:, 2], bias[:, 1:2, :].to_broadcast([P, C, F]), ALU.add))
                            dve.wait_ge(s_out[rt % 2], it * (M // 2 * 16) + rt // 2 * 16 + 16)
                            nc.vector.tensor_tensor(result[:, rt % 2], tmp[:, 1], own_resid, ALU.add).then_inc(s_result, 1)
                            dve.wait_ge(s_result, it * M + rt + 1)
                            nc.vector.memset(small[:, 0, 0:1], 0.0).then_inc(s_final, 1)
                    if sweep == 2:
                        dve.wait_ge(s_kept, it * M + (2 * NB + M + 2))
                        for n, (banks, done) in enumerate(((HIGH, s_high), (LOW, s_low))):
                            dve.wait_ge(s_late, it * 2 + n + 1)
                            for k in banks:
                                part = partial[:, bass.ds(it * M + k, 1), :]
                                last = nc.vector.tensor_tensor(part, part, late_banks[k].unsqueeze(1), ALU.add)
                            last.then_inc(done, 1)
                    assert chain["n"] == M * STEPS[sweep], (sweep, chain["n"])


def kernel(x, adj, L0_gnn_weight, L0_gnn_bias, L1_gnn_kernel, L1_gnn_bias):
    import numpy as np
    import concourse.bacc as bacc
    from concourse.bass_utils import run_bass_kernel_spmd

    n, f = x.shape
    p, c = 128, 4
    b = p * c
    x_laid = np.ascontiguousarray(np.asarray(x).reshape(n // p, p, f).transpose(1, 0, 2))
    adj_laid = np.ascontiguousarray(np.asarray(adj).reshape(n // b, b, n // b, c, p).transpose(0, 2, 4, 3, 1))\
        .reshape((n // b) ** 2 * p, c, b)
    arrays = {"x": x_laid, "adj_blocks": adj_laid, "cheb_weight": np.ascontiguousarray(L0_gnn_weight),
              "cheb_bias": np.ascontiguousarray(L0_gnn_bias), "hyp_kernel": np.ascontiguousarray(L1_gnn_kernel),
              "hyp_bias": np.ascontiguousarray(L1_gnn_bias)}
    nc = bacc.Bacc("TRN2", target_bir_lowering=False, num_devices=1)
    args = [nc.dram_tensor(k, a.shape, mybir.dt.from_np(a.dtype), kind="ExternalInput").ap() for k, a in arrays.items()]
    args.append(nc.dram_tensor("out", x_laid.shape, mybir.dt.float32, kind="ExternalOutput").ap())
    chebyshev_hyperbolic_kernel(nc, *args)
    r = run_bass_kernel_spmd(nc, [arrays], core_ids=[0])
    got = r.results[0]["out"]
    return np.ascontiguousarray(got.transpose(1, 0, 2)).reshape(n, f)
```

```python
import concourse.bass as bass
from concourse import mybir
from contextlib import ExitStack


def chebyshev_hyperbolic_kernel(nc, x, adj_blocks, cheb_weight, cheb_bias, hyp_kernel, hyp_bias, out):
    fp32 = mybir.dt.float32
    bf16 = mybir.dt.bfloat16
    ALU = mybir.AluOpType
    ACT = mybir.ActivationFunctionType
    AX = mybir.AxisListType

    P = 128
    F = x.shape[2]
    CHUNKS = x.shape[1]
    C = 4
    BLOCK = C * P
    NB = CHUNKS // C
    M = 4
    NM = NB // M
    SWEEPS = 4
    LAST = SWEEPS - 1
    LN_EPS = 1e-5
    EPS = 1e-8
    MAX_NORM = 10.0
    MAX_RADIUS = 0.999
    SERIES_BELOW = 0.25

    H, T1, T2, XP = range(4)
    LEFT = [H, T1, T2, XP]
    SINGLE, PAIR, LATE, DIAG, AGAIN, EXTRA = range(6)
    DIAGONALS = 2

    DOWN = [True, False, True, True]

    def macro_of(sweep, it):
        return it if DOWN[sweep] else NM - 1 - it

    def row_in_macro(sweep, rt):
        return rt if DOWN[sweep] else M - 1 - rt

    def row_index(sweep, it, rt):
        if sweep == LAST:
            return (NM - 1 - rt) * M + it
        return macro_of(sweep, it) * M + row_in_macro(sweep, rt)

    def near_before_far(sweep, rt):
        r = row_in_macro(sweep, rt)
        columns = range(M - 1, r + 1, -1) if sweep == 1 else range(r - 1)
        singles = [(r, j, SINGLE) for j in range(r + 1, M)] if sweep == 0 else []
        return [(r, j, PAIR) for j in columns] + singles

    def near_after_far(sweep, rt):
        r = row_in_macro(sweep, rt)
        again = [(r - 1, r - 1, AGAIN)] if sweep == 0 else []
        own = [(r, r, DIAG)] if sweep != 1 else []
        return again + own + ([(r, r + (1 if sweep == 1 else -1), PAIR)] if rt > 0 else [])

    def after_row(sweep, rt):
        return [(rt - 1, rt - 1, AGAIN)] if sweep == 2 and rt > 0 else []

    def closing(sweep):
        if sweep != 2:
            return []
        return [(k, j, LATE) for j in range(1, M - 1) for k in range(j)] + \
            [(M - 1, M - 1, AGAIN)] + [(k, M - 1, LATE) for k in reversed(range(M - 1))]

    def groups_in_row(sweep, it):
        return {0: NM - 1, 1: it, 2: it + it // 2}[sweep]

    def last_groups(rt):
        return rt - 1 if rt > 1 else rt

    def triangle(it):
        return it * it // 3

    def uses_before(sweep, it, slot):
        def near(sweep):
            parts = [closing(sweep)] + [part(sweep, rt) for rt in range(M) for part in (near_before_far, near_after_far)]
            n = sum(kind not in (DIAG, AGAIN) for blocks in parts for _, _, kind in blocks)
            return -(-(n - slot) // M)

        if sweep == 0:
            return it * (near(0) + M * (NM - 1))
        start = NM * (near(0) + M * (NM - 1))
        for before in range(1, sweep):
            start = start + NM * near(before) + M * sum(groups_in_row(before, k) for k in range(NM))
        if sweep == LAST:
            return start + it * sum(last_groups(rt) for rt in range(NM))
        return start + it * near(sweep) + triangle(it) * M + (it // 3 * M if sweep == 2 else 0)

    def nothing():
        pass

    def visitor(e, sweep, it, ring, block):
        def visit(groups, macro_row, place, mt, col, kind, offset=0):
            if kind in (DIAG, AGAIN):
                slot = M + col % DIAGONALS
                row = it * M + (col // DIAGONALS * DIAGONALS)
                uses = e.snap(sweep // 2 * NB + row + (1 if kind == AGAIN else 0))
                block(slot, uses, macro_row, place, mt, col, kind)
                return
            position = ring["position"] + offset
            slot = position % M
            uses = e.snap(ring["before"][slot] + groups + position // M)
            e.compute_val(uses + 1)
            block(slot, uses, macro_row, place, mt, col, kind)
        return visit

    def blocks_of_row(e, sweep, it, rt, ring, block, after_first, at_end):
        visit = visitor(e, sweep, it, ring, block)

        def far(start, end, nth, groups, macro_row, place, kind, after_first=nothing):
            with e.Fori(start, end) as g:
                mt = nc.s_assert_within(nth(g), 0, NM - 1, skip_runtime_bounds_check_because=
                                        "the far columns end at the last macro column")
                for k in range(M):
                    visit(groups + g, macro_row, place, mt, k if DOWN[sweep] else M - 1 - k, kind, k)
                    if k == 0:
                        after_first()

        def near(parts, groups):
            for place, col, kind in parts:
                if col < 0:
                    with e.If(it > 0):
                        visit(groups, macro_of(sweep, it), place, it, col, kind)
                else:
                    visit(groups, macro_of(sweep, it), place, it, col, kind)
                if kind not in (DIAG, AGAIN):
                    ring["position"] += 1

        if sweep == LAST:
            count, groups = last_groups(rt), sum(last_groups(r) for r in range(rt))
            if count > 0:
                far(0, 1, lambda g: g + (NM - count), groups, NM - 1 - rt, it, SINGLE)
            after_first()
            if count > 1:
                far(1, count, lambda g: g + (NM - count), groups, NM - 1 - rt, it, SINGLE)
            at_end()
            return
        in_row = groups_in_row(sweep, it)
        groups = in_row * rt
        first = near_before_far(sweep, rt)
        near(first[:1], groups)
        if first:
            after_first()
        near(first[1:], groups)
        macro_row, place = macro_of(sweep, it), row_in_macro(sweep, rt)
        if sweep == 0:
            done = groups
            for count, nth, kind in [(it, lambda g: g, PAIR), (NM - 1 - it, lambda g: it + 1 + g, SINGLE)]:
                with e.If(count > 0):
                    far(0, count, nth, done, macro_row, place, kind)
                done = done + it
        else:
            turn_here = nothing if first else after_first
            if not first and rt > 0:
                with e.If(it < 1):
                    after_first()
            with e.If(it > 0 if sweep == 1 else it == 1):
                far(0, 1, lambda g: g, groups, macro_row, place, PAIR, turn_here)
            if sweep == 1:
                with e.If(it > 1):
                    far(1, it, lambda g: g, groups, macro_row, place, PAIR)
            else:
                with e.If(it > 1):
                    above, column = (nc.s_assert_within(it - d, 0, NM - 1, skip_runtime_bounds_check_because="it > 1")
                                     for d in (2, 1))
                    for k in range(M):
                        visit(groups, macro_row, place, 0, k, PAIR, 2 * k)
                        if k == 0:
                            turn_here()
                        visit(groups, above, place, column, k, EXTRA, 2 * k + 1)
                    far(1, it, lambda g: g, groups + 1, macro_row, place, PAIR)
        near(near_after_far(sweep, rt), groups + in_row)
        at_end()
        near(after_row(sweep, rt), groups + in_row)

    def closing_blocks(e, sweep, it, ring, block, after_first):
        visit = visitor(e, sweep, it, ring, block)
        for n, (place, col, kind) in enumerate(closing(sweep)):
            visit(groups_in_row(sweep, it) * M, macro_of(sweep, it), place, it, col, kind)
            if kind != AGAIN:
                ring["position"] += 1
            if n == 0:
                after_first()

    def iterations(e, sweep, row, close):
        with e.Fori(0, NM) as it:
            ring = {"position": 0, "before": [e.snap(uses_before(sweep, it, s)) for s in range(M)]}
            for rt in range(M):
                row(it, rt, ring)
            if closing(sweep):
                close(it, ring)

    def last_again(e, block):
        visitor(e, 0, NM, {}, block)(0, NM, -1, NM, -1, AGAIN)

    ctx = ExitStack()
    with ctx:
        def sb(name, shape, dt=fp32):
            return ctx.enter_context(nc.sbuf_tensor(name, shape, dt))

        def pb(name, shape):
            return ctx.enter_context(nc.psum_tensor(name, shape, fp32))

        def sem(name):
            return ctx.enter_context(nc.semaphore(name))

        nodes = sb("nodes", [P, CHUNKS, 4, F])
        resid = sb("resid", [P, CHUNKS, F])
        ring_a = sb("ring_a", [P, M, C, BLOCK])
        diagonals = sb("diagonals", [P, DIAGONALS, C, BLOCK])
        staged_w = sb("staged_w", [P, M + DIAGONALS, C, 2 * F])
        partial = sb("partial", [P, NB, BLOCK])
        acc = sb("acc", [P, BLOCK])
        h_turned = sb("h_turned", [F, BLOCK])
        ident = sb("ident", [P, P])
        zeros = sb("zeros", [P, BLOCK], bf16)
        w_raw = sb("w_raw", [P, 5, F])
        w_term = sb("w_term", [P, 4, F])
        turn = sb("turn", [P, 3, 2 * F])
        bias = sb("bias", [P, 2, F])
        tmp = sb("tmp", [P, 4, C, F])
        squares = sb("squares", [P, 2, C])
        roots = sb("roots", [P, 2, C])
        small = sb("small", [P, 12, C])
        result = sb("result", [P, 2, C, F])

        bank_a = [pb(f"bank_a{i}", [P, BLOCK]) for i in range(2)]
        bank_b = [pb(f"bank_b{i}", [P, BLOCK]) for i in range(2)]
        turned = [pb(f"turned{i}", [P, C, 2 * F]) for i in range(2)]
        h_bank = pb("h_bank", [P, BLOCK])
        extra_bank = pb("extra_bank", [P, BLOCK])
        late_banks = [h_bank[:, :], turned[1][:, :, :].rearrange("p c n -> p (c n)"), bank_a[0][:, :], bank_b[0][:, :]]
        HIGH, LOW = (2, 3), (0, 1)

        s_x = [sem(f"x_landed{i}") for i in range(NM)]
        s_w = sem("weights_landed")
        s_ident0 = sem("ident_zeroed")
        s_const = sem("constants_ready")
        s_terms = sem("weight_terms_ready")
        s_weights = sem("weights_ready")
        s_landed = [sem(f"block_landed{i}") for i in range(M + DIAGONALS)]
        s_staged = [sem(f"weights_staged{i}") for i in range(M + DIAGONALS)]
        s_used = [sem(f"slot_used{i}") for i in range(M + DIAGONALS)]
        s_h = sem("h_ready")
        s_acc = sem("row_accumulated")
        s_evac = sem("row_evacuated")
        s_kept = sem("row_kept")
        s_turned = sem("row_turned_back")
        s_read = sem("turned_read")
        s_final = sem("row_final")
        s_hturned = sem("h_turned")
        s_hready = sem("h_turned_ready")
        s_again = sem("diagonal_added")
        s_late = sem("late_accumulated")
        s_high = sem("late_high_added")
        s_low = sem("late_low_added")
        s_extra = sem("extra_accumulated")
        s_extra_added = sem("extra_added")
        s_var = sem("variance_ready")
        s_std = sem("deviation_ready")
        s_square = sem("norm_squared_ready")
        s_root = sem("norm_root_ready")
        s_norm = sem("norm_ready")
        s_func = sem("function_ready")
        s_chain = sem("vector_chain")
        s_result = sem("result_ready")
        s_out = [sem(f"result_stored{i}") for i in range(2)]

        block = ctx.enter_context(nc.Block())

        def done_before(sweep, it, rt):
            return sweep * NB + it * M + rt

        def order(sweep, mt, off):
            return mt * M + (off if DOWN[sweep] else M - 1 - off) + 1

        def block_in(slot):
            return ring_a[:, slot, :, :] if slot < M else diagonals[:, slot - M, :, :]

        @block.sync
        def _(sp):
            for sweep in range(SWEEPS):
                def load(slot, uses, macro_row, place, mt, col, kind):
                    if kind == AGAIN:
                        return
                    at = sp.snap(((macro_row * M + place) * NB + macro_of(sweep, mt) * M + col) * P)
                    sp.compute_val(at)
                    sp.wait_ge(s_const, 1)
                    sp.wait_ge(s_used[slot], uses + (1 if slot < M else 2))
                    sp.dma_start(block_in(slot), adj_blocks[bass.ds(at, P), :, :])\
                        .then_inc(s_landed[slot], 16)

                iterations(sp, sweep,
                           lambda it, rt, ring: blocks_of_row(sp, sweep, it, rt, ring, load, nothing, nothing),
                           lambda it, ring: closing_blocks(sp, sweep, it, ring, load, nothing))

        @block.gpsimd
        def _(pool):
            nc.gpsimd.memset(zeros[:, :], 0.0)
            nc.gpsimd.memset(ident[:, :], 0.0).then_inc(s_ident0, 1)
            pool.wait_ge(s_ident0, 1)
            nc.gpsimd.affine_select(out=ident[:, :], in_=ident[:, :], compare_op=ALU.not_equal, fill=1.0,
                                    base=0, pattern=[[-1, P]], channel_multiplier=1).then_inc(s_const, 1)

            for s in s_staged[M:]:
                pool.sem_inc(s, 1)
            for sweep in range(SWEEPS):
                def stage(slot, uses, macro_row, place, mt, col, kind):
                    J = pool.snap(nc.s_assert_within(macro_of(sweep, mt) * M + col, 0, NB - 1,
                                                     skip_runtime_bounds_check_because=
                                                     "column -1 is the macro column's before, and there is one"))
                    left = LEFT[sweep] + (1 if kind in (LATE, AGAIN, EXTRA) else 0)
                    width = 2 if kind == PAIR else 1
                    if sweep == 0 and kind in (SINGLE, DIAG):
                        known, count = s_h, order(sweep, mt, col) + 1
                    elif kind in (SINGLE, DIAG):
                        known, count = s_final, sweep * NB + 1
                    else:
                        known, count = s_final, sweep * NB + order(sweep, mt, col) + 1
                    pool.compute_val(count)
                    pool.wait_ge(s_const, 1)
                    pool.wait_ge(known, count)
                    pool.wait_ge(s_used[slot], uses + (1 if slot < M else 2))
                    nc.gpsimd.tensor_copy(
                        staged_w[:, slot, :, 0:width * F].rearrange("p c (w f) -> p c w f", w=width),
                        nodes[:, bass.ds(J * C, C), left:left + width, :]).then_inc(s_staged[slot], 1)

                iterations(pool, sweep,
                           lambda it, rt, ring: blocks_of_row(pool, sweep, it, rt, ring, stage, nothing, nothing),
                           lambda it, ring: closing_blocks(pool, sweep, it, ring, stage, nothing))
                if sweep == 0:
                    last_again(pool, stage)

        @block.tensor
        def _(pe):
            for s in s_used + s_used[M:] + [s_turned, s_high, s_extra_added]:
                pe.sem_inc(s, 1)
            pe.wait_ge(s_const, 1)

            def turn_row(sweep, it, rt):
                rows = done_before(sweep, it, rt)
                pe.wait_ge(s_evac, rows + 3)
                if sweep == LAST:
                    pe.wait_ge(s_read, LAST * NB + 2)
                if sweep > 0 or rt > 0:
                    pe.wait_ge(s_read, rows + 1)
                else:
                    pe.wait_ge(s_read, rows + 2)
                if sweep == 2:
                    out_of, weight = turned[0][:, :, rt % 2 * F:(rt % 2 + 1) * F], w_term[:, 3, :]
                else:
                    out_of, weight = turned[rt % 2][:, :, :], turn[:, min(sweep, 2), :]
                if sweep == 0:
                    pe.wait_ge(s_weights, 1)
                for c in range(C):
                    last = nc.tensor.matmul(out_of[:, c, :], acc[:, c * P:(c + 1) * P], weight,
                                            start=c == 0, stop=True, skip_group_check=True)
                if sweep == 0:
                    pe.wait_ge(s_hready, rows + 2)
                    for c in range(C):
                        last = nc.tensor.matmul(out_of[:, c, F:2 * F], h_turned[:, c * P:(c + 1) * P],
                                                w_term[0:F, 0, :], start=False, stop=True, skip_group_check=True)
                last.then_inc(s_turned, 1)

            def multiply_late(it, slot, uses, place, col):
                if place == col:
                    if place in LOW:
                        pe.wait_ge(s_low, it + 1)
                        pe.wait_ge(s_read, 2 * NB + 2)
                    else:
                        rows = done_before(2, it, 2)
                        pe.wait_ge(s_evac, rows + 3)
                        pe.wait_ge(s_kept, rows + 3)
                if slot < M:
                    pe.wait_ge(s_staged[slot], uses + 1)
                    pe.wait_ge(s_landed[slot], uses * 16 + 16)
                else:
                    pe.wait_ge(s_staged[slot], uses + 2)
                for c in range(C):
                    q = (c % 2) * F
                    last = nc.tensor.matmul(late_banks[place][q:q + F, :], staged_w[:, slot, c, 0:F],
                                            block_in(slot)[:, c, :], start=place == col and c < 2, stop=False,
                                            skip_group_check=True)
                last.then_inc(s_used[slot], 1)
                if (place, col) in ((HIGH[0], M - 1), (LOW[0], M - 1)):
                    for k in HIGH if place in HIGH else LOW:
                        last = nc.tensor.matmul(late_banks[k][:, 0:16], zeros[:, 0:P], zeros[:, 0:16],
                                                start=False, stop=True, skip_group_check=True)
                    last.then_inc(s_late, 1)

            def multiply_extra(it, rt, slot, uses, col):
                if col == 0:
                    pe.wait_ge(s_extra_added, it // 3 * M + (rt + 1))
                pe.wait_ge(s_staged[slot], uses + 1)
                pe.wait_ge(s_landed[slot], uses * 16 + 16)
                for c in range(C):
                    q = (c % 2) * F
                    last = nc.tensor.matmul(extra_bank[q:q + F, :], staged_w[:, slot, c, 0:F], block_in(slot)[:, c, :],
                                            start=col == 0 and c < 2, stop=False, skip_group_check=True)
                last.then_inc(s_used[slot], 1)
                if col == M - 1:
                    nc.tensor.matmul(extra_bank[:, 0:16], zeros[:, 0:P], zeros[:, 0:16], start=False, stop=True,
                                     skip_group_check=True).then_inc(s_extra, 1)

            def multiply_again(slot, uses, col):
                pe.wait_ge(s_staged[slot], uses + 2)
                bank = bank_a[col % 2]
                for c in range(C):
                    q = (c % 2) * F
                    last = nc.tensor.matmul(bank[q:q + F, :], staged_w[:, slot, c, 0:F], block_in(slot)[:, c, :],
                                            start=c == 0, stop=False, skip_group_check=True)
                last.then_inc(s_used[slot], 1)
                nc.tensor.matmul(bank[:, 0:16], zeros[:, 0:P], zeros[:, 0:16], start=False, stop=True,
                                 skip_group_check=True).then_inc(s_again, 1)

            for sweep in range(SWEEPS):
                def row(it, rt, ring):
                    rows = pe.snap(done_before(sweep, it, rt))
                    a, b = bank_a[rt % 2], bank_b[rt % 2]
                    pe.wait_ge(s_evac, rows + 1)
                    if sweep != LAST:
                        pe.wait_ge(s_kept, rows + 1)
                    if sweep == 2 and rt == 0:
                        pe.wait_ge(s_high, it + 1)
                    if sweep == LAST and rt < 2:
                        pe.wait_ge(s_high, NM + 1)
                        pe.wait_ge(s_low, NM + 1)
                    for bank in ((a, b), (a,), (a,), (b,))[sweep]:
                        nc.tensor.matmul(bank[:, :], zeros[:, 0:P], zeros[:, :], start=True, stop=False,
                                         skip_group_check=True)

                    def multiply(slot, uses, macro_row, place, mt, col, kind):
                        if kind == EXTRA:
                            multiply_extra(it, rt, slot, uses, col)
                            return
                        if kind == AGAIN and sweep == 0:
                            multiply_again(slot, uses, col)
                            return
                        if kind == AGAIN:
                            multiply_late(it, slot, uses, place, col)
                            return
                        if sweep == 0 and kind == DIAG:
                            pe.compute_val(rows + 1)
                            pe.compute_val(uses + 2)
                            pe.wait_ge(s_const, 1)
                        pe.wait_ge(s_staged[slot], uses + (1 if slot < M else 2))
                        if sweep == 0 and kind == DIAG:
                            pe.wait_ge(s_hready, rows + 1)
                            for c in range(C):
                                last = nc.tensor.transpose(h_bank[0:F, c * P:(c + 1) * P],
                                                           staged_w[:, slot, c, 0:F], ident[:, :])
                            last.then_inc(s_hturned, 1)
                        if slot < M:
                            pe.wait_ge(s_landed[slot], uses * 16 + 16)
                        else:
                            pe.wait_ge(s_landed[slot], uses * 8 + 16)
                        for c in range(C):
                            if kind == PAIR:
                                last = nc.tensor.matmul(a[:, :], staged_w[:, slot, c, :], ring_a[:, slot, c, :],
                                                        start=False, stop=False, skip_group_check=True)
                            else:
                                q = (c % 2) * F
                                last = nc.tensor.matmul(b[q:q + F, :], staged_w[:, slot, c, 0:F],
                                                        block_in(slot)[:, c, :],
                                                        start=sweep == 2 and c < 2,
                                                        stop=False, skip_group_check=True)
                        last.then_inc(s_used[slot], 1)

                    def turn_previous():
                        if rt > 0:
                            turn_row(sweep, it, rt - 1)
                        elif sweep < 2:
                            with pe.If(it > 0):
                                turn_row(sweep, it, -1)

                    def complete():
                        for bank in ((a, b), (a,), (a, b), (b,))[sweep]:
                            last = nc.tensor.matmul(bank[:, 0:16], zeros[:, 0:P], zeros[:, 0:16], start=False, stop=True,
                                                    skip_group_check=True)
                        last.then_inc(s_acc, 1)

                    blocks_of_row(pe, sweep, it, rt, ring, multiply, turn_previous, complete)
                    if rt == M - 1 and sweep == LAST:
                        turn_row(sweep, it, rt)

                def close(it, ring):
                    def late(slot, uses, macro_row, place, mt, col, kind):
                        multiply_late(it, slot, uses, place, col)
                    closing_blocks(pe, sweep, it, ring, late, lambda: turn_row(sweep, it, M - 1))

                iterations(pe, sweep, row, close)
                if sweep < 2:
                    turn_row(sweep, NM, -1)
                if sweep == 0:
                    last_again(pe, lambda slot, uses, macro_row, place, mt, col, kind: multiply_again(slot, uses, col))

        @block.scalar
        def _(act):
            for s in s_out:
                act.sem_inc(s, 16)
            for m in range(NM):
                n = CHUNKS // NM
                act.dma_start(resid[:, m * n:(m + 1) * n, :], x[:, m * n:(m + 1) * n, :]).then_inc(s_x[m], 16)
            loads = [(bias[:, 0, :], cheb_bias.partition_broadcast(P)), (bias[:, 1, :], hyp_bias.partition_broadcast(P))]
            for part in (slice(0, F), slice(F, P)):
                loads += [(w_raw[part, 0:4, :], cheb_weight.rearrange("k i o -> i k o")), (w_raw[part, 4, :], hyp_kernel)]
            for dst, src in loads:
                act.dma_start(dst, src).then_inc(s_w, 16)

            with act.Fori(0, NB // 2) as k:
                act.wait_ge(s_var, k + 1)
                nc.scalar.activation(roots[:, :, :], squares[:, :, :], ACT.Sqrt).then_inc(s_std, 1)

            def keep(sweep, it, rt):
                i = act.snap(row_index(sweep, it, rt))
                if sweep == 0:
                    act.wait_ge(s_again, it * M + (rt + 1))
                    part = slice(0, P)
                else:
                    act.wait_ge(s_evac, done_before(sweep, it, rt) + 3)
                    part = slice(F, P)
                nc.scalar.activation(partial[part, bass.ds(i, 1), :], bank_a[rt % 2][part, :].unsqueeze(1),
                                     ACT.Copy).then_inc(s_kept, 1)

            for sweep in (0, 1):
                with act.Fori(0, NM) as it:
                    for rt in range(M):
                        keep(sweep, it, rt)
            with act.Fori(0, NM) as it:
                for rt in range(M):
                    t = act.snap(it * M + rt)
                    keep(2, it, rt)
                    act.wait_ge(s_var, t + (NB // 2 + 1))
                    nc.scalar.activation(roots[:, :, :], squares[:, :, :], ACT.Sqrt).then_inc(s_std, 1)
                    act.wait_ge(s_norm, t + 1)
                    nc.scalar.activation(small[:, 4, :], small[:, 3, :], ACT.Tanh).then_inc(s_func, 1)
                    nc.scalar.activation(small[:, 5, :], ident[:, 0:C], ACT.Sqrt)
            with act.Fori(0, NM) as it:
                for rt in range(M):
                    t = act.snap(it * M + rt)
                    act.wait_ge(s_square, t + 1)
                    nc.scalar.activation(small[:, 10, :], small[:, 7, :], ACT.Sqrt).then_inc(s_root, 1)
                    act.wait_ge(s_norm, t + NB + 1)
                    nc.scalar.activation(small[:, 4, :], small[:, 3, :], ACT.Ln, bias=1.0, scale=1.0)
                    nc.scalar.activation(small[:, 5, :], small[:, 3, :], ACT.Ln, bias=1.0, scale=-1.0)\
                        .then_inc(s_func, 1)
                    act.wait_ge(s_result, t + 1)
                    row_at = act.snap(row_index(LAST, it, rt) * C)
                    act.dma_start(out[:, bass.ds(row_at, C), :], result[:, rt % 2, :, :]).then_inc(s_out[rt % 2], 16)
            for s in s_out:
                act.wait_ge(s, NB // 2 * 16 + 16)

        @block.vector
        def _(dve):
            def over_f(v):
                return v.unsqueeze(2).to_broadcast([P, C, F])

            def step(chain, ins):
                chain["n"] += 1
                ins.then_inc(s_chain, 1)
                dve.wait_ge(s_chain, chain["base"] + chain["n"])

            LN_STEPS = 5
            LN_STEPS = 5
            STEPS = [2, 1, 11, 18]
            starts = [NB // 2 * LN_STEPS]
            for n in STEPS[:-1]:
                starts.append(starts[-1] + NB * n)

            def centred(chain, v, dst, total):
                step(chain, nc.vector.tensor_reduce(total, v, AX.X, ALU.add))
                return nc.vector.scalar_tensor_tensor(
                    dst, total.unsqueeze(2).to_broadcast(list(v.shape)), 1.0 / F, v, ALU.mult, ALU.subtract, reverse1=True)

            for s in (s_h, s_final, s_hready, s_low):
                dve.sem_inc(s, 1)
            for s in (s_evac, s_kept, s_read):
                dve.sem_inc(s, 2)
            pair, pair_sq = (tmp[:, k:k + 2].rearrange("p k c f -> p (k c) f") for k in (0, 2))
            square_sums, std = (v[:, :, :].rearrange("p k c -> p (k c)") for v in (squares, roots))
            rstd = small[:, 0:2, :].rearrange("p k c -> p (k c)")
            for m in range(NM):
                dve.wait_ge(s_x[m], 16)
                with dve.Fori(0, M // 2) as k:
                    nth = dve.snap(k + m * (M // 2))
                    chain = {"n": 0, "base": dve.snap(nth * LN_STEPS)}
                    at = dve.snap(nth * (2 * C))
                    dve.wait_ge(s_h, nth * 2 + 1)
                    step(chain, centred(chain, resid[:, bass.ds(at, 2 * C), :], pair, rstd))
                    step(chain, nc.vector.tensor_tensor(pair_sq, pair, pair, ALU.mult))
                    step(chain, nc.vector.tensor_reduce(square_sums, pair_sq, AX.X, ALU.add))
                    nc.vector.tensor_scalar(square_sums, square_sums, 1.0 / F, LN_EPS, ALU.mult, ALU.add)\
                        .then_inc(s_var, 1)
                    dve.wait_ge(s_std, nth + 1)
                    step(chain, nc.vector.reciprocal(rstd, std))
                    nc.vector.scalar_tensor_tensor(nodes[:, bass.ds(at, 2 * C), H, :], pair, 0.0,
                                                   rstd.unsqueeze(2).to_broadcast([P, 2 * C, F]), ALU.max, ALU.mult)\
                        .then_inc(s_h, 2)
            dve.wait_ge(s_const, 1)
            dve.wait_ge(s_w, 6 * 16)
            nc.vector.tensor_tensor(w_term[:, 0:2, :], w_raw[:, 0:2, :], w_raw[:, 2:4, :], ALU.subtract)\
                .then_inc(s_terms, 1)
            nc.vector.tensor_scalar(w_term[:, 2:4, :], w_raw[:, 2:4, :], 2.0, None, ALU.mult).then_inc(s_terms, 1)
            dve.wait_ge(s_terms, 2)
            nc.vector.tensor_copy(turn[:, 0:2, F:2 * F], w_term[:, 1:3, :])
            nc.vector.tensor_copy(turn[:, 2, F:2 * F], w_raw[:, 4, :])
            nc.vector.tensor_tensor(turn[:, :, 0:F], ident[:, 0:F].unsqueeze(1).to_broadcast([P, 3, F]),
                                    ident[:, F:P].unsqueeze(1).to_broadcast([P, 3, F]), ALU.add)\
                .then_inc(s_weights, 1)

            for sweep in range(SWEEPS):
                with dve.Fori(0, NM) as it:
                    chain = {"n": 0, "base": dve.snap(starts[sweep] + it * (M * STEPS[sweep]))}
                    for rt in range(M):
                        rows = dve.snap(done_before(sweep, it, rt))
                        at = dve.snap(row_index(sweep, it, rt) * C)
                        dve.compute_val(at)
                        own = [nodes[:, bass.ds(at, C), q, :] for q in range(4)]
                        own_resid = resid[:, bass.ds(at, C), :]
                        if sweep == 2:
                            projected = turned[0][:, :, rt % 2 * F:(rt % 2 + 1) * F]
                        else:
                            row_sum, projected = turned[rt % 2][:, :, 0:F], turned[rt % 2][:, :, F:2 * F]

                        i = dve.snap(row_index(sweep, it, rt))
                        dve.compute_val(i)

                        if sweep == 0:
                            dve.wait_ge(s_hturned, rows + 1)
                            nc.vector.tensor_copy(h_turned[:, :], h_bank[0:F, :]).then_inc(s_hready, 1)

                        if sweep == 2:
                            with dve.If(it > 1):
                                above = nc.s_assert_within(it * M + (rt - 2 * M), 0, NB - 1,
                                                           skip_runtime_bounds_check_because="it > 1")
                                part = partial[:, bass.ds(above, 1), :]
                                dve.wait_ge(s_high, it + 1)
                                dve.wait_ge(s_low, it + 1)
                                dve.wait_ge(s_extra, it // 3 * M + (rt + 1))
                                nc.vector.tensor_tensor(part, part, extra_bank[:, :].unsqueeze(1), ALU.add)\
                                    .then_inc(s_extra_added, 1)
                        dve.wait_ge(s_acc, rows + 1)
                        dve.wait_ge(s_turned, rows + 1)
                        if sweep != 0:
                            dve.wait_ge(s_kept, sweep * NB + 2)
                        bank = bank_b[rt % 2]
                        if sweep == LAST:
                            dve.wait_ge(s_high, NM + 1)
                            dve.wait_ge(s_low, NM + 1)
                            dve.wait_ge(s_extra_added, 2 * M + 1)
                        own_part = partial[:, bass.ds(i, 1), :]
                        if sweep == 0:
                            step(chain, nc.vector.tensor_copy(acc[:, :], bank[:, :]))
                        elif sweep == LAST:
                            nc.vector.tensor_tensor(acc[:, :].unsqueeze(1), own_part, bank[:, :].unsqueeze(1),
                                                    ALU.add).then_inc(s_evac, 1)
                        elif sweep == 1:
                            nc.vector.tensor_copy(acc[F:P, :].unsqueeze(1), own_part[F:P])
                            nc.vector.tensor_tensor(acc[0:F, :].unsqueeze(1), own_part[0:F],
                                                    bank_a[rt % 2][0:F, :].unsqueeze(1), ALU.add).then_inc(s_evac, 1)
                        else:
                            nc.vector.tensor_copy(acc[0:F, :], bank[0:F, :])
                            step(chain, nc.vector.tensor_tensor(acc[F:P, :].unsqueeze(1), own_part[F:P],
                                                                bank[F:P, :].unsqueeze(1), ALU.add))
                        if sweep in (0, 2):
                            nc.vector.tensor_tensor(acc[0:F, :], acc[0:F, :], bank_a[rt % 2][0:F, :], ALU.add)\
                                .then_inc(s_evac, 1)
                        dve.wait_ge(s_turned, rows + 2)
                        dve.wait_ge(s_final, rows + 1)
                        dve.wait_ge(s_read, rows + 2)
                        if sweep == 0:
                            nc.vector.tensor_copy(own[T1], row_sum).then_inc(s_final, 1)
                            step(chain, nc.vector.tensor_tensor(
                                tmp[:, 0], projected, bias[:, 0:1, :].to_broadcast([P, C, F]), ALU.add))
                            nc.vector.tensor_tensor(own_resid, own_resid, tmp[:, 0], ALU.add).then_inc(s_read, 1)
                        if sweep == 1:
                            nc.vector.scalar_tensor_tensor(own[T2], row_sum, 2.0, own[H], ALU.mult, ALU.subtract)\
                                .then_inc(s_final, 1)
                            nc.vector.tensor_tensor(own_resid, own_resid, projected, ALU.add).then_inc(s_read, 1)
                            step(chain, nc.vector.tensor_copy(own_part[0:F], zeros[0:F, :].unsqueeze(1)))
                        if sweep == 2:
                            nc.vector.tensor_tensor(own_resid, own_resid, projected, ALU.add).then_inc(s_read, 1)
                            dve.compute_val(rows + 3)
                            dve.wait_ge(s_const, 1)
                            dve.wait_ge(s_read, rows + 3)
                            v = tmp[:, 2]
                            step(chain, centred(chain, own_resid, v, small[:, 0, :]))
                            nc.vector.tensor_tensor(tmp[:, 0], v, v, ALU.mult)
                            step(chain, nc.vector.scalar_tensor_tensor(tmp[:, 1], v, 0.0, v, ALU.max, ALU.mult))
                            step(chain, nc.vector.tensor_reduce(square_sums, tmp[:, 0:2].rearrange("p k c f -> p (k c) f"),
                                                                AX.X, ALU.add))
                            nc.vector.tensor_scalar(squares[:, 0, :], squares[:, 0, :], 1.0 / F, LN_EPS,
                                                    ALU.mult, ALU.add).then_inc(s_var, 1)
                            dve.wait_ge(s_std, it * M + (rt + NB // 2 + 1))
                            norm, func, rstd, ratio = small[:, 3, :], small[:, 4, :], small[:, 1, :], small[:, 6, :]
                            step(chain, nc.vector.reciprocal(rstd, roots[:, 0, :]))
                            step(chain, nc.vector.tensor_tensor(ratio, roots[:, 1, :], rstd, ALU.mult))
                            nc.vector.tensor_scalar(norm, ratio, MAX_NORM, None, ALU.min).then_inc(s_norm, 1)
                            dve.wait_ge(s_norm, it * M + rt + 1)
                            step(chain, nc.vector.tensor_scalar(small[:, 7, :], norm, EPS, None, ALU.add))
                            step(chain, nc.vector.reciprocal(small[:, 8, :], small[:, 7, :]))
                            step(chain, nc.vector.tensor_tensor(ratio, small[:, 8, :], rstd, ALU.mult))
                            dve.wait_ge(s_func, it * M + rt + 1)
                            step(chain, nc.vector.tensor_tensor(small[:, 9, :], func, ratio, ALU.mult))
                            nc.vector.scalar_tensor_tensor(own[XP], v, 0.0, over_f(small[:, 9, :]), ALU.max, ALU.mult)\
                                .then_inc(s_final, 1)
                        if sweep == LAST:
                            radius, log_up, log_down = small[:, 3, :], small[:, 4, :], small[:, 5, :]
                            sq, series, mask, ratio = small[:, 6, :], small[:, 7, :], small[:, 8, :], small[:, 9, :]
                            step(chain, nc.vector.tensor_copy(tmp[:, 0], row_sum))
                            step(chain, nc.vector.tensor_tensor(tmp[:, 1], tmp[:, 0], tmp[:, 0], ALU.mult))
                            nc.vector.tensor_reduce(small[:, 7, :], tmp[:, 1], AX.X, ALU.add).then_inc(s_square, 1)
                            dve.wait_ge(s_root, it * M + rt + 1)
                            nc.vector.tensor_scalar(radius, small[:, 10, :], MAX_RADIUS, None, ALU.min)\
                                .then_inc(s_norm, 1)
                            dve.wait_ge(s_norm, NB + it * M + rt + 1)
                            step(chain, nc.vector.tensor_tensor(sq, radius, radius, ALU.mult))
                            step(chain, nc.vector.tensor_scalar(series, sq, 1.0 / 13, None, ALU.mult))
                            for k in (11, 9, 7, 5, 3):
                                step(chain, nc.vector.scalar_tensor_tensor(series, series, 1.0 / k, sq,
                                                                           ALU.add, ALU.mult))
                            step(chain, nc.vector.scalar_tensor_tensor(series, series, 1.0, radius, ALU.add, ALU.mult))
                            nc.vector.tensor_scalar(mask, radius, SERIES_BELOW, None, ALU.is_ge)
                            dve.wait_ge(s_func, NB + it * M + rt + 1)
                            step(chain, nc.vector.tensor_tensor(ratio, log_up, log_down, ALU.subtract))
                            step(chain, nc.vector.scalar_tensor_tensor(ratio, ratio, 0.5, series, ALU.mult, ALU.subtract))
                            step(chain, nc.vector.tensor_tensor(ratio, ratio, mask, ALU.mult))
                            step(chain, nc.vector.tensor_tensor(ratio, ratio, series, ALU.add))
                            step(chain, nc.vector.tensor_scalar(small[:, 11, :], radius, EPS, None, ALU.add))
                            step(chain, nc.vector.reciprocal(small[:, 10, :], small[:, 11, :]))
                            step(chain, nc.vector.tensor_tensor(ratio, ratio, small[:, 10, :], ALU.mult))
                            nc.vector.tensor_tensor(tmp[:, 2], projected, over_f(ratio), ALU.mult).then_inc(s_read, 1)
                            dve.wait_ge(s_read, rows + 3)
                            step(chain, nc.vector.tensor_tensor(
                                tmp[:, 1], tmp[:, 2], bias[:, 1:2, :].to_broadcast([P, C, F]), ALU.add))
                            dve.wait_ge(s_out[rt % 2], it * (M // 2 * 16) + rt // 2 * 16 + 16)
                            nc.vector.tensor_tensor(result[:, rt % 2], tmp[:, 1], own_resid, ALU.add).then_inc(s_result, 1)
                            dve.wait_ge(s_result, it * M + rt + 1)
                            nc.vector.memset(small[:, 0, 0:1], 0.0).then_inc(s_final, 1)
                    if sweep == 2:
                        dve.wait_ge(s_kept, it * M + (2 * NB + M + 2))
                        for n, (banks, done) in enumerate(((HIGH, s_high), (LOW, s_low))):
                            dve.wait_ge(s_late, it * 2 + n + 1)
                            for k in banks:
                                part = partial[:, bass.ds(it * M + k, 1), :]
                                last = nc.vector.tensor_tensor(part, part, late_banks[k].unsqueeze(1), ALU.add)
                            last.then_inc(done, 1)
                    assert chain["n"] == M * STEPS[sweep], (sweep, chain["n"])


def kernel(x, adj, L0_gnn_weight, L0_gnn_bias, L1_gnn_kernel, L1_gnn_bias):
    import numpy as np
    import concourse.bacc as bacc
    from concourse.bass_utils import run_bass_kernel_spmd

    n, f = x.shape
    p, c = 128, 4
    b = p * c
    x_laid = np.ascontiguousarray(np.asarray(x).reshape(n // p, p, f).transpose(1, 0, 2))
    adj_laid = np.ascontiguousarray(np.asarray(adj).reshape(n // b, b, n // b, c, p).transpose(0, 2, 4, 3, 1))\
        .reshape((n // b) ** 2 * p, c, b)
    arrays = {"x": x_laid, "adj_blocks": adj_laid, "cheb_weight": np.ascontiguousarray(L0_gnn_weight),
              "cheb_bias": np.ascontiguousarray(L0_gnn_bias), "hyp_kernel": np.ascontiguousarray(L1_gnn_kernel),
              "hyp_bias": np.ascontiguousarray(L1_gnn_bias)}
    nc = bacc.Bacc("TRN2", target_bir_lowering=False, num_devices=1)
    args = [nc.dram_tensor(k, a.shape, mybir.dt.from_np(a.dtype), kind="ExternalInput").ap() for k, a in arrays.items()]
    args.append(nc.dram_tensor("out", x_laid.shape, mybir.dt.float32, kind="ExternalOutput").ap())
    chebyshev_hyperbolic_kernel(nc, *args)
    r = run_bass_kernel_spmd(nc, [arrays], core_ids=[0])
    got = r.results[0]["out"]
    return np.ascontiguousarray(got.transpose(1, 0, 2)).reshape(n, f)
```
